# Optimizing a Trainium2 kernel written in Bass

```python
import numpy as np
import jax
import jax.numpy as jnp

def _softmax(x, axis=-1):
    return jax.nn.softmax(x, axis=axis)

def _gelu(x):
    return jax.nn.gelu(x, approximate=True)

def _silu(x):
    return jax.nn.silu(x)

def _sigmoid(x):
    return jax.nn.sigmoid(x)

def _layernorm(x, axis=-1, eps=1e-05):
    m = jnp.mean(x, axis=axis, keepdims=True)
    v = jnp.var(x, axis=axis, keepdims=True)
    return (x - m) / jnp.sqrt(v + eps)

def _scatter_add(tgt, idx, src, axis=0):
    return tgt.at[idx].add(src)

def _segment_sum(src, seg, n):
    return jax.ops.segment_sum(src, seg, n)
kernel_name = 'mk_seq_preln_d1_jaxref_r4_21166e'

def setup_inputs(seed: int=0):
    np.random.seed(seed)
    _w = jnp.asarray

    def _L0_attn_setup():
        import jax, jax.numpy as jnp
        import numpy as np
        N_EMBED = 512
        N_HEAD = 16
        HEAD_DIM = N_EMBED // N_HEAD
        BATCH, SEQ = (2, 512)

        def _rotate_half(t):
            d = t.shape[-1] // 2
            x1, x2 = (t[..., :d], t[..., d:])
            return jnp.concatenate([-x2, x1], axis=-1)
        key = jax.random.key(seed)
        k1, k2, k3 = jax.random.split(key, 3)
        x = jax.random.normal(k1, (BATCH, SEQ, N_EMBED), dtype=jnp.float32)
        w_attn = jax.random.normal(k2, (N_EMBED, (N_HEAD + 2) * HEAD_DIM), dtype=jnp.float32) * N_EMBED ** (-0.5)
        w_out = jax.random.normal(k3, (N_EMBED, N_EMBED), dtype=jnp.float32) * N_EMBED ** (-0.5)
        return {'x': x, 'w_attn': w_attn, 'w_out': w_out}
    _L0_attn_in = _L0_attn_setup()

    def _L0_ffn_setup():
        import jax, jax.numpy as jnp
        import numpy as np
        SEQ, BS, D, F, E = (256, 2, 512, 512, 8)
        key = jax.random.key(seed)
        ks = jax.random.split(key, 8)
        s = 0.02
        return {'hidden_states': jax.random.normal(ks[0], (SEQ, BS, D), jnp.float32), 'router_w': jax.random.normal(ks[1], (D, E), jnp.float32) * s, 'gate_w': jax.random.normal(ks[2], (E, D, F), jnp.float32) * s, 'up_w': jax.random.normal(ks[3], (E, D, F), jnp.float32) * s, 'down_w': jax.random.normal(ks[4], (E, F, D), jnp.float32) * s, 'shared_gate_w': jax.random.normal(ks[5], (D, F), jnp.float32) * s, 'shared_up_w': jax.random.normal(ks[6], (D, F), jnp.float32) * s, 'shared_down_w': jax.random.normal(ks[7], (F, D), jnp.float32) * s}
    _L0_ffn_in = _L0_ffn_setup()
    _d = {'L0_attn_x': _L0_attn_in['x'], 'L0_attn_w_attn': _L0_attn_in['w_attn'], 'L0_attn_w_out': _L0_attn_in['w_out'], 'L0_ffn_router_w': _L0_ffn_in['router_w'], 'L0_ffn_gate_w': _L0_ffn_in['gate_w'], 'L0_ffn_up_w': _L0_ffn_in['up_w'], 'L0_ffn_down_w': _L0_ffn_in['down_w'], 'L0_ffn_shared_gate_w': _L0_ffn_in['shared_gate_w'], 'L0_ffn_shared_up_w': _L0_ffn_in['shared_up_w'], 'L0_ffn_shared_down_w': _L0_ffn_in['shared_down_w']}
    _x0 = _d['L0_attn_x']
    _d['L0_attn_x'] = jax.random.normal(jax.random.fold_in(jax.random.key(seed), 1), (8, 512, 512), dtype=_x0.dtype)
    del _x0
    return _d

def reference(L0_attn_x, L0_attn_w_attn, L0_attn_w_out, L0_ffn_router_w, L0_ffn_gate_w, L0_ffn_up_w, L0_ffn_down_w, L0_ffn_shared_gate_w, L0_ffn_shared_up_w, L0_ffn_shared_down_w):

    def _L0_attn_ref(x, w_attn, w_out):
        import jax, jax.numpy as jnp
        import numpy as np
        N_EMBED = 512
        N_HEAD = 16
        HEAD_DIM = N_EMBED // N_HEAD
        BATCH, SEQ = (2, 512)

        def _rotate_half(t):
            d = t.shape[-1] // 2
            x1, x2 = (t[..., :d], t[..., d:])
            return jnp.concatenate([-x2, x1], axis=-1)
        B, T, E = x.shape
        H, hd = (N_HEAD, HEAD_DIM)
        qkv = x @ w_attn
        q = qkv[..., :H * hd].reshape(B, T, H, hd).transpose(0, 2, 1, 3)
        k = qkv[..., H * hd:(H + 1) * hd].reshape(B, T, 1, hd).transpose(0, 2, 1, 3)
        v = qkv[..., (H + 1) * hd:].reshape(B, T, 1, hd).transpose(0, 2, 1, 3)
        pos = 10000.0 ** ((-2.0 * jnp.arange(0, hd, 2, dtype=jnp.float32) - 1.0) / hd)
        angles = jnp.arange(T, dtype=jnp.float32)[:, None] * pos[None, :]
        rot = jnp.concatenate([angles, angles], axis=-1)
        cos, sin = (jnp.cos(rot), jnp.sin(rot))
        q = q * cos + _rotate_half(q) * sin
        k = k * cos + _rotate_half(k) * sin
        scores = jnp.matmul(q, jnp.swapaxes(k, -1, -2)) * hd ** (-0.5)
        attn = jax.nn.softmax(scores, axis=-1)
        out = jnp.matmul(attn, v)
        out = out.transpose(0, 2, 1, 3).reshape(B, T, E)
        return out @ w_out

    def _L0_ffn_ref(hidden_states, router_w, gate_w, up_w, down_w, shared_gate_w, shared_up_w, shared_down_w):
        import jax, jax.numpy as jnp
        import numpy as np
        SEQ, BS, D, F, E = (256, 2, 512, 512, 8)
        S, B, Dm = hidden_states.shape
        x = hidden_states.reshape(-1, Dm)
        logits = x @ router_w
        expert_idx = jnp.argmax(logits, axis=-1)
        score = jax.nn.sigmoid(jnp.max(logits, axis=-1))
        xs = x * score[:, None]
        n_experts = router_w.shape[1]
        out = jnp.zeros_like(x)
        for e in range(n_experts):
            m = (expert_idx == e)[:, None]
            xe = jnp.where(m, xs, 0.0)
            h = jax.nn.silu(xe @ gate_w[e]) * (xe @ up_w[e])
            out = out + jnp.where(m, h @ down_w[e], 0.0)
        shared = jax.nn.silu(x @ shared_gate_w) * (x @ shared_up_w) @ shared_down_w
        return (out + shared).reshape(S, B, Dm)
    x = L0_attn_x
    x = x + _L0_attn_ref(_layernorm(x, axis=-1), L0_attn_w_attn, L0_attn_w_out)
    x = x + _L0_ffn_ref(_layernorm(x, axis=-1), L0_ffn_router_w, L0_ffn_gate_w, L0_ffn_up_w, L0_ffn_down_w, L0_ffn_shared_gate_w, L0_ffn_shared_up_w, L0_ffn_shared_down_w)
    return x

_drawn_inputs = setup_inputs


def setup_inputs(seed=0):
    import zlib

    import numpy as np

    out = dict(_drawn_inputs(seed))
    spreads = {}
    factors = {'L0_ffn_router_w': 2.862,
     'L0_ffn_gate_w': 2.704,
     'L0_ffn_up_w': 2.676,
     'L0_ffn_down_w': 2.676}
    for name, (base, spread) in spreads.items():
        noise = np.random.default_rng([zlib.crc32(name.encode()), seed]).standard_normal(out[name].shape)
        drawn = base * np.exp(spread * noise) if base else spread * noise
        out[name] = jnp.asarray(drawn.astype(out[name].dtype))
    for name, factor in factors.items():
        out[name] = (out[name] * factor).astype(out[name].dtype)
    return out
```

```python
import concourse.bass as bass
from concourse import mybir
from contextlib import ExitStack

F32 = mybir.dt.float32
F32R = mybir.dt.float32r
BF16 = mybir.dt.bfloat16
I32 = mybir.dt.int32
U32 = mybir.dt.uint32
ALU = mybir.AluOpType
ACT = mybir.ActivationFunctionType
AX = mybir.AxisListType

P = 128
B, T, D = 8, 512, 512
H, HD = 16, 32
KC = D // P
TT = T // P
GH = P // HD
G = H // GH
NQ = 1 + G
QKV = NQ * P
SCALE = HD ** -0.5
EPS = 1e-5
SROWS = 3 * HD + 1
HALF_SWAP = [(i + HD // 2) % HD for i in range(HD)]


def static_zero(b):
    return isinstance(b, int) and b == 0


class Counter:

    def __init__(self, sem, per):
        self.sem, self.per = sem, per

    def wait(self, eng, b, k):
        v = b * self.per + k
        if not isinstance(v, int) or v > 0:
            eng.wait_ge(self.sem, v)


RING = 3
USES = {"A": KC + NQ, "C": TT, "T": H * KC}
PER_BANK = {s: [len(range(k, n, RING)) for k in range(RING)] for s, n in USES.items()}


def ring_count(stage, b, u, bank=None):
    k = u % RING if bank is None else bank
    a, c, t = (PER_BANK[s][k] for s in "ACT")
    whole = a + c + t
    here = len(range(k, u + 1, RING))
    if stage == "A":
        return here if static_zero(b) else b * whole - c + here
    if stage == "C":
        return (b + 1) * whole - c + (0 if isinstance(b, int) and b == B - 1 else a) + here
    return b * whole + a + here


def ring_wait(eng, sems, stage, b, u):
    eng.wait_ge(sems[u % RING], ring_count(stage, b, u))


def ring_take(eng, free, stage, b, u):
    n = ring_count(stage, b, u) - 1
    if not isinstance(n, int) or n > 0:
        eng.wait_ge(free[u % RING], n)


def ring_wait_all(eng, sems, stage, b, u):
    for k in range(RING):
        eng.wait_ge(sems[k], ring_count(stage, b, u, k))


def products(pe, out, pairs):
    terms = [(a, c) for (a, _), (c, _) in pairs] + [(l, c) for (_, l), (c, _) in pairs] + \
            [(a, m) for (a, _), (_, m) in pairs]
    for n, (a, c) in enumerate(terms):
        last = pe.matmul(out, a, c, start=n == 0, stop=n == len(terms) - 1)
    return last


def attention(nc, x, w_attn, w_out, rope, q_dram, x1):
    with ExitStack() as ctx:
        def sb(name, shape, dt=F32):
            return ctx.enter_context(nc.sbuf_tensor(name, shape, dt))

        def sem(name):
            return ctx.enter_context(nc.semaphore(name))

        wq_hi = sb("wq_hi", [P, KC, QKV], F32R)
        wq_lo = sb("wq_lo", [P, KC, QKV], F32R)
        wo_hi = sb("wo_hi", [P, KC, D], F32R)
        wo_lo = sb("wo_lo", [P, KC, D], F32R)
        cos_sin = sb("cos_sin", [P, 2, T])
        ident = sb("ident", [P, P])
        ones = sb("ones", [P, HD])
        exponent = sb("exponent", [P, TT])
        xa = sb("xa", [P, TT, D])
        xT_hi = sb("xT_hi", [P, KC, T], F32R)
        xT_lo = sb("xT_lo", [P, KC, T], F32R)
        stats = sb("stats", [P, TT, 6])
        mv = sb("mv", [P, TT, 2])
        vareps = sb("vareps", [P, TT])
        rstd = sb("rstd", [P, TT])
        q_raw = sb("q_raw", [P, T])
        q_cos = sb("q_cos", [P, T])
        q_swap = sb("q_swap", [P, T])
        q_rot = sb("q_rot", [P, T])
        q_hi = sb("q_hi", [P, 2, T], F32R)
        q_lo = sb("q_lo", [P, 2, T], F32R)
        q_stack = sb("q_stack", [SROWS, H, T], F32R)
        k_stack = sb("k_stack", [SROWS, T], F32R)
        valT = sb("valT", [P, T])
        val = sb("val", [P, TT, HD])
        maxes = sb("maxes", [P, H * TT])
        neg_max = sb("neg_max", [GH * TT, P], F32R)
        probs = sb("probs", [P, 2 * GH, KC, T])
        psums = sb("psums", [P, GH, T])
        ptemp = sb("ptemp", [P, T])
        recip = sb("recip", [P, T])
        mark = sb("mark", [P, 1])
        o_all = sb("o_all", [P, G, T])
        xres = sb("xres", [P, 2, D])

        ps_s = ctx.enter_context(nc.psum_tensor("ps_s", [P, 2, T], F32))
        ps_ring = ctx.enter_context(nc.psum_tensor("ps_ring", [P, RING, 512], F32))
        ps_o = ctx.enter_context(nc.psum_tensor("ps_o", [P, T], F32))
        ps_sum = ctx.enter_context(nc.psum_tensor("ps_sum", [P, T], F32))
        ps_x = ctx.enter_context(nc.psum_tensor("ps_x", [P, 512], F32))

        RAW = (H + 2) * HD
        raw_q = probs[:, 0:2 * GH, :, :].rearrange("p h c t -> p (h c t)")[:, 0:KC * RAW] \
            .rearrange("p (c n) -> p c n", c=KC)
        raw_o = probs[:, 0:2 * GH, :, :].rearrange("p h c t -> p (h c t)")[:, GH * KC * T:GH * KC * T + KC * D] \
            .rearrange("p (c n) -> p c n", c=KC)

        raw_q_in, raw_o_in, rope_in = sem("raw_q_in"), sem("raw_o_in"), sem("rope_in")
        const_ok, ones_ok = sem("const_ok"), sem("ones_ok")
        w_hi_ok, w_lo_ok = sem("w_hi_ok"), sem("w_lo_ok")
        x_in = Counter(sem("x_in"), 16)
        ln_stats = Counter(sem("ln_stats"), 2 * TT + 1)
        ln_rstd = Counter(sem("ln_rstd"), 1)
        ln_done = Counter(sem("ln_done"), TT)
        full = [sem(f"ring_full{k}") for k in range(RING)]
        free = [sem(f"ring_free{k}") for k in range(RING)]
        xt_hi = Counter(sem("xt_hi"), KC)
        xt_lo = Counter(sem("xt_lo"), KC)
        raw_ok = Counter(sem("raw_ok"), NQ)
        swap_ok = Counter(sem("swap_ok"), NQ)
        sin_ok = Counter(sem("sin_ok"), NQ)
        rot_ok = Counter(sem("rot_ok"), NQ)
        hi_ok = Counter(sem("hi_ok"), NQ)
        k_ok = Counter(sem("k_ok"), 2)
        lo_ok = Counter(sem("lo_ok"), NQ)
        q_out = [Counter(sem(f"q_out{k}"), 32 * (G // 2)) for k in range(2)]
        q_in = [Counter(sem(f"q_in{g}"), 16 * 3) for g in range(G)]
        x_full = Counter(sem("x_full"), 1 + G)
        x_free = Counter(sem("x_free"), 1 + G)
        s_full = Counter(sem("s_full"), H * TT)
        s_free = Counter(sem("s_free"), H * TT)
        shift_in = Counter(sem("shift_in"), 16 * G)
        pair_ok = Counter(sem("pair_ok"), 2 * H)
        psum_ok = Counter(sem("psum_ok"), H)
        pv_done = Counter(sem("pv_done"), G * KC)
        sum_done = Counter(sem("sum_done"), G)
        rec_ok = Counter(sem("rec_ok"), G * TT)
        o_ok = Counter(sem("o_ok"), G)
        oT_hi = Counter(sem("oT_hi"), G)
        oT_lo = Counter(sem("oT_lo"), G)
        xr_in = [Counter(sem(f"xr_in{k}"), 16 * TT // 2) for k in range(2)]
        x1_out = [Counter(sem(f"x1_out{k}"), 16 * TT // 2) for k in range(2)]

        block = ctx.enter_context(nc.Block())

        def batches(eng, batch):
            batch(0, True, False)
            with eng.Fori(1, B - 1) as b:
                batch(b, False, False)
            batch(B - 1, False, True)

        def slot_stored(eng, b, n):
            q_out[n % 2].wait(eng, b, 32 * max(0, (n - 1) // 2))

        @block.sync
        def _(sp):
            def load_x(b, first):
                if not first:
                    ring_wait(sp, full, "A", b - 1, KC - 1)
                sp.dma_start(xa[:, :, :], x[bass.ds(b, 1), :, :].rearrange("b (t p) d -> p (b t) d", p=P)) \
                    .then_inc(x_in.sem, 16)

            def load_residual(b, t):
                if t >= 2:
                    x1_out[t % 2].wait(sp, b, 16 * (t // 2))
                sp.dma_start(xres[:, t % 2, :], x[bass.ds(b, 1), t * P:(t + 1) * P, :]
                             .rearrange("b p d -> (b p) d")).then_inc(xr_in[t % 2].sem, 16)

            def store_x1(b, t):
                ring_wait(sp, free, "C", b, t)
                sp.dma_start(x1[bass.ds(b * T + t * P, P), :],
                             xres[:, t % 2, :]).then_inc(x1_out[t % 2].sem, 16)

            def stack(b, first):
                for g in range(G):
                    n = g + 1
                    for part, ok, i in ((q_hi, hi_ok, 0), (q_lo, lo_ok, 1)):
                        ok.wait(sp, b, n + 1)
                        sp.dma_start(q_dram[bass.ds(b, 1), g, i, :, :].rearrange("b p t -> (b p) t"),
                                     part[:, n % 2, :].bitcast(F32)).then_inc(q_out[n % 2].sem, 16)
                    q_out[n % 2].wait(sp, b, 32 * ((n - 1) // 2 + 1))
                    for r, i in enumerate((0, 1, 0)):
                        sp.dma_start(q_stack[r * HD:(r + 1) * HD, g * GH:(g + 1) * GH, :].bitcast(F32),
                                     q_dram[bass.ds(b, 1), g, i, :, :]
                                     .rearrange("b (j d) t -> d (b j) t", j=GH)).then_inc(q_in[g].sem, 16)

            def batch(b, first, last):
                if not last:
                    load_x(b + 1, False)
                if not first:
                    load_residual(b - 1, 0)
                    load_residual(b - 1, 1)
                stack(b, first)
                if not first:
                    for t in range(TT):
                        store_x1(b - 1, t)
                        if t + 2 < TT:
                            load_residual(b - 1, t + 2)
                for g in range(G):
                    shifts_ok, stored = x_free.per * b + 1 + g + 1, x1_out[0].per * b
                    if g == G - 1 and not first:
                        if not isinstance(b, int):
                            shifts_ok, stored = sp.snap(shifts_ok), sp.snap(stored)
                        for k in range(2):
                            sp.wait_ge(x1_out[k].sem, stored)
                    sp.wait_ge(x_free.sem, shifts_ok)
                    sp.dma_start(q_stack[SROWS - 1:SROWS, g * GH:(g + 1) * GH, :].bitcast(F32), neg_max[:, :].bitcast(F32)) \
                        .then_inc(shift_in.sem, 16)

            sp.dma_start(raw_q, w_attn.rearrange("(c p) n -> p c n", p=P)).then_inc(raw_q_in, 16)
            load_x(0, True)
            sp.dma_start(cos_sin[:, :, :], rope).then_inc(rope_in, 16)
            sp.dma_start(raw_o, w_out.rearrange("(c p) n -> p c n", p=P)).then_inc(raw_o_in, 16)
            batches(sp, batch)
            load_residual(B - 1, 0)
            load_residual(B - 1, 1)
            for t in range(TT):
                store_x1(B - 1, t)
                if t + 2 < TT:
                    load_residual(B - 1, t + 2)
            for k in range(2):
                x1_out[k].wait(sp, B, 0)

        @block.gpsimd
        def _(pool):
            pool.memset(ident[:, :], 0.0).then_inc(const_ok, 1)
            pool.wait_ge(const_ok, 1)
            pool.affine_select(out=ident[:, :], in_=ident[:, :], compare_op=ALU.not_equal, fill=1.0,
                               base=0, pattern=[[-1, P]], channel_multiplier=1).then_inc(const_ok, 1)
            pool.memset(ones[:, :], 1.0).then_inc(const_ok, 1)
            pool.memset(exponent[:, :], -0.5).then_inc(const_ok, 1)

            def rstd_of(b):
                ln_stats.wait(pool, b, 2 * TT + 1)
                ln_done.wait(pool, b, 0)
                pool.tensor_tensor(rstd[:, :], vareps[:, :], exponent[:, :], ALU.pow).then_inc(ln_rstd.sem, 1)

            def rotate(b, n):
                swap_ok.wait(pool, b, n + 1)
                pool.tensor_tensor(q_swap[:, :], q_swap[:, :], cos_sin[:, 1, :], ALU.mult).then_inc(sin_ok.sem, 1)
                sin_ok.wait(pool, b, n + 1)
                ring_wait(pool, free, "A", b, KC + n)
                lo_ok.wait(pool, b, n)
                pool.tensor_tensor(q_rot[:, :], q_cos[:, :], q_swap[:, :], ALU.add).then_inc(rot_ok.sem, 1)

            def sum_chunks(b, h):
                slot, j = h % (2 * GH), h % GH
                ring_wait_all(pool, free, "T", b, h * KC + KC - 1)
                sum_done.wait(pool, b, h // GH)
                psum_ok.wait(pool, b, h)
                pool.tensor_tensor(psums[:, j, :], probs[:, slot, 0, :], probs[:, slot, 1, :],
                                   ALU.add).then_inc(pair_ok.sem, 1)
                pool.tensor_tensor(ptemp[:, :], probs[:, slot, 2, :], probs[:, slot, 3, :],
                                   ALU.add).then_inc(pair_ok.sem, 1)
                pair_ok.wait(pool, b, 2 * (h + 1))
                pool.tensor_tensor(psums[:, j, :], psums[:, j, :], ptemp[:, :], ALU.add).then_inc(psum_ok.sem, 1)

            def batch(b, first, last):
                for n in range(NQ):
                    rotate(b, n)
                for h in range(H):
                    sum_chunks(b, h)
                    if h == 3 * GH - 1 and not last:
                        rstd_of(b + 1)

            pool.wait_ge(const_ok, 4)
            rstd_of(0)
            pool.wait_ge(rope_in, 16)
            batches(pool, batch)

        @block.scalar
        def _(act):
            def copy(out, in_, scale=1.0):
                return act.activation(out, in_, ACT.Copy, scale=scale)

            KV = H * HD
            act.wait_ge(raw_q_in, 16)
            for r in range(3):
                copy(wq_hi[:, :, r * HD:(r + 1) * HD], raw_q[:, :, KV:KV + HD]).then_inc(w_hi_ok, 1)
            copy(wq_hi[:, :, 3 * HD:P], raw_q[:, :, KV + HD:KV + 2 * HD]).then_inc(w_hi_ok, 1)
            copy(wq_hi[:, :, P:QKV], raw_q[:, :, 0:KV]).then_inc(w_hi_ok, 1)
            act.wait_ge(raw_o_in, 16)
            copy(wo_hi[:, :, :], raw_o).then_inc(w_hi_ok, 1)

            def transposed(b, first):
                if not first:
                    act.wait_ge(full[(TT - 1) % RING], ring_count("C", b - 2, TT - 1))
                for c in range(KC):
                    ring_wait(act, full, "A", b, c)
                    copy(xT_hi[:, c, :], ps_ring[:, c % RING, :]).then_inc(xt_hi.sem, 1)

            def raw(b, n):
                ring_wait(act, full, "A", b, KC + n)
                if n == 0:
                    x_full.wait(act, b, 0)
                    copy(valT[:, :], ps_ring[:, (KC + n) % RING, :]).then_inc(k_ok.sem, 1)
                swap_ok.wait(act, b, n)
                copy(q_raw[:, :], ps_ring[:, (KC + n) % RING, :]).then_inc(raw_ok.sem, 1)

            def high(b, n):
                rot_ok.wait(act, b, n + 1)
                slot_stored(act, b, n)
                lo_ok.wait(act, b, max(0, n - 1))
                if n == 0:
                    pv_done.wait(act, b, 0)
                    copy(k_stack[0:2 * HD, :], q_rot[0:2 * HD, :]).then_inc(k_ok.sem, 1)
                    copy(q_hi[2 * HD:3 * HD, 0, :], q_rot[2 * HD:3 * HD, :]).then_inc(hi_ok.sem, 1)
                else:
                    copy(q_hi[:, n % 2, :], q_rot[:, :]).then_inc(hi_ok.sem, 1)

            def outputs(b):
                for g in range(G):
                    o_ok.wait(act, b, g + 1)
                    copy(xT_hi[:, g, :], o_all[:, g, :]).then_inc(oT_hi.sem, 1)

            def values(b):
                x_full.wait(act, b, 1)
                copy(val[:, :, :], ps_x[:, :].rearrange("p (t d) -> p t d", d=P)[:, :, 3 * HD:P]).then_inc(x_free.sem, 1)

            def shifts(b, g):
                x_full.wait(act, b, 1 + g + 1)
                shift_in.wait(act, b, 16 * g)
                copy(neg_max[:, :], ps_x[0:GH * TT, 0:P], scale=-1.0).then_inc(x_free.sem, 1)

            def exps(b, h, first):
                if not (first and h < 2 * GH) and h % GH == 0:
                    pv_done.wait(act, b, (h // GH - 1) * KC)
                    psum_ok.wait(act, b, (h // GH - 1) * GH)
                for c in range(KC):
                    u = h * KC + c
                    ring_wait(act, full, "T", b, u)
                    act.activation(probs[:, h % (2 * GH), c, :], ps_ring[:, u % RING, :], ACT.Exp,
                                   scale=SCALE).then_inc(free[u % RING], 1)

            def batch(b, first, last):
                transposed(b, first)
                for n in range(NQ):
                    raw(b, n)
                    if 1 <= n < NQ - 1:
                        high(b, n - 1)
                if not first:
                    outputs(b - 1)
                high(b, NQ - 2)
                high(b, NQ - 1)
                values(b)
                shifts(b, 0)
                for h in range(H):
                    exps(b, h, first)
                    if h % GH == 0 and h // GH + 1 < G:
                        shifts(b, h // GH + 1)

            act.wait_ge(w_lo_ok, 6)
            batches(act, batch)
            outputs(B - 1)

        @block.vector
        def _(dve):
            def minus(out, a, b):
                return dve.tensor_tensor(out, a, b.bitcast(F32), ALU.subtract)

            def normalise_stats(b):
                x_in.wait(dve, b, 16)
                for t in range(TT):
                    dve.bn_stats(stats[:, t, :], xa[:, t, :]).then_inc(ln_stats.sem, 1)
                ln_stats.wait(dve, b, TT)
                dve.memset(mark[:, :], 0.0)
                for t in range(TT):
                    dve.bn_aggr(mv[:, t, :], stats[:, t, :]).then_inc(ln_stats.sem, 1)
                ln_stats.wait(dve, b, 2 * TT)
                dve.tensor_scalar(vareps[:, :], mv[:, :, 1], EPS, None, ALU.add).then_inc(ln_stats.sem, 1)

            def normalise(b):
                ln_rstd.wait(dve, b, 1)
                for t in range(TT):
                    dve.tensor_scalar(xa[:, t, :], xa[:, t, :], mv[:, t, 0:1], rstd[:, t:t + 1],
                                      ALU.subtract, ALU.mult).then_inc(ln_done.sem, 1)

            dve.memset(k_stack[SROWS - 1:SROWS, :].bitcast(F32), 1.0).then_inc(ones_ok, 1)
            normalise_stats(0)
            normalise(0)
            KV = H * HD
            dve.wait_ge(w_hi_ok, 6)
            for r in range(3):
                minus(wq_lo[:, :, r * HD:(r + 1) * HD], raw_q[:, :, KV:KV + HD],
                      wq_hi[:, :, r * HD:(r + 1) * HD]).then_inc(w_lo_ok, 1)
            minus(wq_lo[:, :, 3 * HD:P], raw_q[:, :, KV + HD:KV + 2 * HD],
                  wq_hi[:, :, 3 * HD:P]).then_inc(w_lo_ok, 1)
            minus(wq_lo[:, :, P:QKV], raw_q[:, :, 0:KV], wq_hi[:, :, P:QKV]).then_inc(w_lo_ok, 1)
            minus(wo_lo[:, :, :], raw_o, wo_hi[:, :, :]).then_inc(w_lo_ok, 1)
            dve.wait_ge(rope_in, 16)

            def transposed(b):
                for c in range(KC):
                    xt_hi.wait(dve, b, c + 1)
                    ring_wait(dve, full, "A", b, c)
                    minus(xT_lo[:, c, :], ps_ring[:, c % RING, :], xT_hi[:, c, :]).then_inc(free[c % RING], 1)

            def swap(b, n):
                rot_ok.wait(dve, b, n)
                raw_ok.wait(dve, b, n + 1)
                dve.tensor_tensor(q_cos[:, :], ps_ring[:, (KC + n) % RING, :], cos_sin[:, 0, :],
                                  ALU.mult).then_inc(free[(KC + n) % RING], 1)
                dve.stream_shuffle(q_swap[:, :], q_raw[:, :], HALF_SWAP).then_inc(swap_ok.sem, 1)

            def low(b, n):
                hi_ok.wait(dve, b, n + 1)
                if n == 0:
                    minus(k_stack[2 * HD:3 * HD, :], q_rot[2 * HD:3 * HD, :],
                          q_hi[2 * HD:3 * HD, 0, :]).then_inc(lo_ok.sem, 1)
                else:
                    minus(q_lo[:, n % 2, :], q_rot[:, :], q_hi[:, n % 2, :]).then_inc(lo_ok.sem, 1)

            def outputs(b):
                for g in range(G):
                    oT_hi.wait(dve, b, g + 1)
                    minus(xT_lo[:, g, :], o_all[:, g, :], xT_hi[:, g, :]).then_inc(oT_lo.sem, 1)

            def residual(b, t):
                xr_in[t % 2].wait(dve, b, 16 * (t // 2 + 1))
                ring_wait(dve, full, "C", b, t)
                dve.tensor_tensor(xres[:, t % 2, :], ps_ring[:, t % RING, :], xres[:, t % 2, :],
                                  ALU.add).then_inc(free[t % RING], 1)

            def head_max(b, h):
                for t in range(TT):
                    n = h * TT + t
                    s_full.wait(dve, b, n + 1)
                    dve.tensor_reduce(maxes[:, n:n + 1], ps_s[:, n % 2, :], AX.X, ALU.max).then_inc(s_free.sem, 1)

            def reciprocals(b, g, quarters):
                sum_done.wait(dve, b, g + 1)
                for q in quarters:
                    cols = slice(q * P, (q + 1) * P)
                    dve.reciprocal(recip[:, cols], ps_sum[:, cols]).then_inc(rec_ok.sem, 1)

            def weigh(b, g):
                rec_ok.wait(dve, b, (g + 1) * TT)
                pv_done.wait(dve, b, (g + 1) * KC)
                oT_hi.wait(dve, b, 0)
                dve.tensor_tensor(o_all[:, g, :], ps_o[:, :], recip[:, :], ALU.mult).then_inc(o_ok.sem, 1)

            def batch(b, first, last):
                transposed(b)
                for n in range(NQ):
                    swap(b, n)
                    if n == NQ - 1 and not first:
                        outputs(b - 1)
                    if n >= 1:
                        low(b, n - 1)
                low(b, NQ - 1)
                for t in range(TT):
                    if not first:
                        residual(b - 1, t)
                    head_max(b, 2 * t)
                    head_max(b, 2 * t + 1)
                for g in range(G + 1):
                    for j in range(GH):
                        if g + 2 < G:
                            head_max(b, (g + 2) * GH + j)
                        if g >= 1 and j == 2:
                            reciprocals(b, g - 1, (0, 1))
                        if g >= 1 and j == 3:
                            reciprocals(b, g - 1, (2, 3))
                            weigh(b, g - 1)
                    if g == 2 and not last:
                        normalise_stats(b + 1)
                    if g == 3 and not last:
                        normalise(b + 1)

            batches(dve, batch)
            outputs(B - 1)
            for t in range(TT):
                residual(B - 1, t)

        @block.tensor
        def _(pe):
            pe.wait_ge(const_ok, 4)
            pe.wait_ge(ones_ok, 1)

            def transposes(b):
                ln_done.wait(pe, b, TT)
                for c in range(KC):
                    ring_take(pe, free, "A", b, c)
                    for t in range(TT):
                        last = pe.transpose(ps_ring[:, c % RING, t * P:(t + 1) * P],
                                            xa[:, t, c * P:(c + 1) * P], ident[:, :])
                    last.then_inc(full[c % RING], 1)

            def project(b):
                xt_hi.wait(pe, b, KC)
                ring_wait_all(pe, free, "A", b, KC - 1)
                for n in range(NQ):
                    u, cols = KC + n, slice(n * P, (n + 1) * P)
                    ring_take(pe, free, "A", b, u)
                    products(pe, ps_ring[:, u % RING, :],
                             [((wq_hi[:, c, cols], wq_lo[:, c, cols]), (xT_hi[:, c, :], xT_lo[:, c, :]))
                              for c in range(KC)]).then_inc(full[u % RING], 1)

            def values(b):
                k_ok.wait(pe, b, 2)
                x_free.wait(pe, b, 0)
                for t in range(TT):
                    last = pe.transpose(ps_x[:, t * P:(t + 1) * P], valT[:, t * P:(t + 1) * P], ident[:, :])
                last.then_inc(x_full.sem, 1)

            def out_tile(b, t):
                if t == 0:
                    oT_hi.wait(pe, b, G)
                    oT_lo.wait(pe, b, G)
                ring_take(pe, free, "C", b, t)
                rows = slice(t * P, (t + 1) * P)
                products(pe, ps_ring[:, t % RING, :],
                         [((xT_hi[:, g, rows], xT_lo[:, g, rows]), (wo_hi[:, g, :], wo_lo[:, g, :]))
                          for g in range(G)]).then_inc(full[t % RING], 1)

            def scores(b, h):
                if h % GH == 0:
                    q_in[h // GH].wait(pe, b, 16 * 3)
                if h == 0:
                    lo_ok.wait(pe, b, 1)
                for t in range(TT):
                    n = h * TT + t
                    s_free.wait(pe, b, n - 1)
                    pe.matmul(ps_s[:, n % 2, :], q_stack[0:3 * HD, h, t * P:(t + 1) * P],
                              k_stack[0:3 * HD, :], start=True, stop=True).then_inc(s_full.sem, 1)

            def max_rows(b, g):
                s_free.wait(pe, b, (g + 1) * GH * TT)
                x_free.wait(pe, b, 1 + g)
                cols = slice(g * GH * TT, (g + 1) * GH * TT)
                pe.transpose(ps_x[0:GH * TT, 0:P], maxes[:, cols], ident[:, :]).then_inc(x_full.sem, 1)

            def scores_by_key(b, h):
                if h % GH == 0:
                    shift_in.wait(pe, b, 16 * (h // GH + 1))
                for c in range(KC):
                    u = h * KC + c
                    ring_take(pe, free, "T", b, u)
                    pe.matmul(ps_ring[:, u % RING, :], k_stack[:, c * P:(c + 1) * P], q_stack[:, h, :],
                              start=True, stop=True).then_inc(full[u % RING], 1)

            def weighted(b, g, c):
                if c == 0:
                    ring_wait_all(pe, free, "T", b, (g + 1) * GH * KC - 1)
                    x_free.wait(pe, b, 1)
                    o_ok.wait(pe, b, g)
                for j in range(GH):
                    last = pe.matmul(ps_o[j * HD:(j + 1) * HD, :], val[:, c, :],
                                     probs[:, (g * GH + j) % (2 * GH), c, :], start=c == 0, stop=c == KC - 1)
                last.then_inc(pv_done.sem, 1)

            def sums(b, g):
                psum_ok.wait(pe, b, (g + 1) * GH)
                rec_ok.wait(pe, b, g * TT)
                for j in range(GH):
                    last = pe.matmul(ps_sum[j * HD:(j + 1) * HD, :], ones[:, :], psums[:, j, :],
                                     start=True, stop=True)
                last.then_inc(sum_done.sem, 1)

            def batch(b, first, last):
                transposes(b)
                project(b)
                values(b)
                for t in range(TT):
                    if not first:
                        out_tile(b - 1, t)
                    scores(b, 2 * t)
                    scores(b, 2 * t + 1)
                max_rows(b, 0)
                for g in range(G + 1):
                    for j in range(GH):
                        if g < G:
                            scores_by_key(b, g * GH + j)
                        if g + 2 < G:
                            scores(b, (g + 2) * GH + j)
                        if j == 0 and g + 1 < G:
                            max_rows(b, g + 1)
                        if g >= 1:
                            weighted(b, g - 1, j)
                        if g >= 1 and j == 1:
                            sums(b, g - 1)

            pe.wait_ge(w_lo_ok, 6)
            batches(pe, batch)
            for t in range(TT):
                out_tile(B - 1, t)


def rope_table():
    import numpy as np
    d = np.arange(P) % HD
    pos = np.float32(10000.0) ** ((np.float32(-2.0) * np.arange(0, HD, 2, dtype=np.float32) - np.float32(1.0))
                                  / np.float32(HD))
    angles = (np.arange(T, dtype=np.float32)[None, :] * pos[d % (HD // 2)][:, None]).astype(np.float32)
    sign = np.where(d < HD // 2, -1.0, 1.0).astype(np.float32)[:, None]
    return np.ascontiguousarray(np.stack([np.cos(angles), np.sin(angles) * sign], axis=1).astype(np.float32))


E, F = 8, 512
NT = B * T // P
ET = NT + E
RING4 = 4
REGION = B * T + P
NULL_ROW = E * REGION
SORTED_ROWS = NULL_ROW + P
ROW = 2 * D + 16
MATS = 3
EULER = 2.718281828459045


def experts(nc, x1, w_router, w_gate, w_up, w_down, ws_gate, ws_up, ws_down, rows, out):
    with ExitStack() as ctx:
        def sb(name, shape, dt=F32):
            return ctx.enter_context(nc.sbuf_tensor(name, shape, dt))

        def ps(name, cols=512):
            return ctx.enter_context(nc.psum_tensor(name, [P, 512], F32))

        def sem(name):
            return ctx.enter_context(nc.semaphore(name))

        w_hi = sb("w_hi", [P, 2, MATS, KC, F], F32R)
        w_lo = sb("w_lo", [P, 2, MATS, KC, F], F32R)
        raw = sb("raw", [P, MATS, KC, F])
        wr = sb("wr", [P, KC, E])
        wr_hi = sb("wr_hi", [P, KC, E], F32R)
        wr_lo = sb("wr_lo", [P, KC, E], F32R)
        identity = sb("identity", [P, P])
        before = sb("before", [P, P], BF16)
        all_ones = sb("all_ones", [P, P], BF16)
        first_wins = sb("first_wins", [P, E])
        region = sb("region", [P, E])
        minus_half = sb("minus_half", [P, 1])
        euler = sb("euler", [P, 1])
        token = sb("token", [P, 1])
        xt = sb("xt", [P, RING4, D])
        xn = sb("xn", [P, RING4, D])
        st = sb("st", [P, RING4, 6])
        mean_var = sb("mean_var", [P, RING4, 2])
        var_eps = sb("var_eps", [P, RING4])
        inv_std = sb("inv_std", [P, RING4])
        x_hi = sb("x_hi", [P, KC, P], F32R)
        x_lo = sb("x_lo", [P, KC, P], F32R)
        h_hi = sb("h_hi", [P, KC, P], F32R)
        h_lo = sb("h_lo", [P, KC, P], F32R)
        silu = sb("silu", [P, F])
        hid = sb("hid", [P, F])
        row = sb("row", [P, RING4, ROW])
        y_out = sb("y_out", [P, RING4, D])
        target = sb("target", [P, RING4], U32)
        logits = sb("logits", [P, E])
        top = sb("top", [P, 1])
        minus_top = sb("minus_top", [P, 1])
        exp_minus = sb("exp_minus", [P, 1])
        denom = sb("denom", [P, 1])
        score = sb("score", [P, 1])
        rank_of = sb("rank_of", [P, E])
        winner = sb("winner", [P, 1])
        chosen = sb("chosen", [P, E], BF16)
        chosen_so_far = sb("chosen_so_far", [P, E], BF16)
        place = sb("place", [P, E])
        place1 = sb("place1", [P, E])
        place_sum = sb("place_sum", [P, 1])
        mark_v = sb("mark_v", [P, 1])
        mark_p = sb("mark_p", [P, RING4 + 2])

        counts = sb("counts", [P, E])
        steps128 = sb("steps128", [P, E, NT])
        over = sb("over", [P, E, NT])
        tiles_of = sb("tiles_of", [P, E])
        tile_end = sb("tile_end", [P, E])
        jump = sb("jump", [P, E])
        tile_no = sb("tile_no", [P, ET, E])
        passed = sb("passed", [P, ET, E])
        weighted_p = sb("weighted_p", [P, ET, E])
        tabf = sb("tabf", [P, 6, ET])
        tab = sb("tab", [P, 5, ET], I32)
        EID, ODD, FIRST, BASE, FETCH, TMP = range(6)
        filler = sb("filler", [P, ROW])
        fill_at = sb("fill_at", [P, E])
        fill_row = sb("fill_row", [P, E], U32)
        lane = sb("lane", [P, 1])

        ps_g, ps_u, ps_xt, ps_ht, ps_y, ps_l, ps_k = (
            ps(f"ps_{n}") for n in ("g", "u", "xt", "ht", "y", "l", "k"))

        raw_in, fetched = sem("raw_in"), sem("fetched")
        wr_in, wr_ok = sem("wr_in"), sem("wr_ok")
        cst, cst_v = sem("cst"), sem("cst_v")
        sh_hi, sh_lo = sem("sh_hi"), sem("sh_lo")
        e_hi, e_lo = sem("e_hi"), sem("e_lo")
        xt_in = [Counter(sem(f"xt_in{k}"), 16) for k in range(RING4)]
        row_io = [Counter(sem(f"row_io{k}"), 16) for k in range(RING4)]
        row_in = [Counter(sem(f"row_in{k}"), 16) for k in range(RING4)]
        y_io = [Counter(sem(f"y_io{k}"), 16) for k in range(RING4)]
        stat_ok = Counter(sem("stat_ok"), 3)
        inv_ok = Counter(sem("inv_ok"), 1)
        xn_ok = Counter(sem("xn_ok"), 1)
        g_full, u_full, x_full, h_full, y_full, l_full, k_full = (
            Counter(sem(f"{n}_full"), 1) for n in ("g", "u", "x", "h", "y", "l", "k"))
        silu_ok, xhi_ok, hhi_ok = (Counter(sem(n), 1) for n in ("silu_ok", "xhi_ok", "hhi_ok"))
        xlo_ok, hlo_ok, hid_ok, y_ok = (Counter(sem(n), 1) for n in ("xlo_ok", "hlo_ok", "hid_ok", "y_ok"))
        route = Counter(sem("route"), 6)
        exp_ok = Counter(sem("exp_ok"), 1)
        score_ok = Counter(sem("score_ok"), 2)
        xs_ok = Counter(sem("xs_ok"), 2)
        placed = Counter(sem("placed"), 5)
        token_ok = Counter(sem("token_ok"), 1)
        carried = Counter(sem("carried"), 1)
        table = sem("table")
        table_ok = sem("table_ok")
        count_ps, fill_io, fill_ok = sem("count_ps"), sem("fill_io"), sem("fill_ok")

        block = ctx.enter_context(nc.Block())

        def tiles(eng, t0, count, step):
            for k in range(RING4):
                step(t0 + k, k, k == 0, False)
            with eng.Fori(t0 // RING4 + 1, (t0 + count) // RING4 - 1) as i:
                for k in range(RING4):
                    step(i * RING4 + k, k, False, False)
            for k in range(RING4):
                step(t0 + count - RING4 + k, k, False, k == RING4 - 1)

        def ring_dma(eng, counters, t, k, done):
            v = (t - k) * (16 // RING4) + 16 * done
            if not isinstance(v, int) or v > 0:
                eng.wait_ge(counters[k].sem, v)

        @block.sync
        def _(sp):
            for m, w in enumerate((ws_gate, ws_up, ws_down)):
                sp.dma_start(raw[:, m, :, :], w.rearrange("(c p) n -> p c n", p=P)).then_inc(raw_in, 16)
            sp.dma_start(wr[:, :, :], w_router.rearrange("(c p) n -> p c n", p=P)).then_inc(wr_in, 16)

            def load_x(t, k, first, last):
                if not isinstance(t, int) or t >= RING4:
                    y_ok.wait(sp, t, 1 - RING4)
                sp.dma_start(xt[:, k, :], x1[bass.ds(t * P, P), :]).then_inc(xt_in[k].sem, 16)

            def load_row(t, k, first, last):
                j = t - NT
                at = sp.value_load(tab[0:1, BASE, bass.ds(j, 1)], min_val=0, max_val=NULL_ROW)
                y_ok.wait(sp, t, 1 - RING4)
                sp.dma_start(row[:, k, :], rows[bass.ds(at, P), :]).then_inc(row_in[k].sem, 16)

            for k in range(RING4):
                load_x(k, k, False, False)
            sp.wait_ge(sh_lo, MATS)
            for m, w in enumerate((w_gate, w_up, w_down)):
                sp.dma_start(raw[:, m, :, :], w[0, :, :].rearrange("(c p) n -> p c n", p=P)).then_inc(raw_in, 16)
            with sp.Fori(1, NT // RING4) as i:
                for k in range(RING4):
                    load_x(i * RING4 + k, k, False, False)
            sp.wait_ge(table_ok, 1)
            for k in range(RING4):
                sp.wait_ge(row_io[k].sem, 16 * (NT // RING4))
            sp.wait_ge(fill_io, 16 * (E + 1))
            tiles(sp, NT, ET, load_row)

        @block.gpsimd
        def _(pool):
            pool.memset(identity[:, :], 0.0).then_inc(cst, 1)
            pool.memset(before[:, :], 1.0).then_inc(cst, 1)
            pool.memset(all_ones[:, :], 1.0).then_inc(cst, 1)
            pool.memset(minus_half[:, :], -0.5).then_inc(cst, 1)
            pool.memset(euler[:, :], EULER).then_inc(cst, 1)
            pool.memset(mark_p[:, :], 0.0).then_inc(cst, 1)
            pool.memset(filler[:, :], 0.0).then_inc(cst, 1)
            pool.wait_ge(cst, 7)
            pool.affine_select(out=identity[:, :], in_=identity[:, :], compare_op=ALU.not_equal, fill=1.0,
                               base=0, pattern=[[-1, P]], channel_multiplier=1).then_inc(cst, 1)
            pool.affine_select(out=before[:, :], in_=before[:, :], compare_op=ALU.is_gt, fill=0.0,
                               base=0, pattern=[[1, P]], channel_multiplier=-1).then_inc(cst, 1)
            pool.iota(first_wins[:, :], [[-1, E]], base=E, channel_multiplier=0,
                      allow_small_or_imprecise_dtypes=True).then_inc(cst, 1)
            pool.iota(region[:, :], [[REGION, E]], base=0, channel_multiplier=0,
                      allow_small_or_imprecise_dtypes=True).then_inc(cst, 1)
            pool.iota(token[:, :], [[0, 1]], base=0, channel_multiplier=1,
                      allow_small_or_imprecise_dtypes=True).then_inc(cst, 1)
            pool.iota(lane[:, :], [[0, 1]], base=0, channel_multiplier=1,
                      allow_small_or_imprecise_dtypes=True).then_inc(cst, 1)
            pool.iota(steps128[:, :, :], [[0, E], [P, NT]], base=0, channel_multiplier=0,
                      allow_small_or_imprecise_dtypes=True).then_inc(cst, 1)
            pool.iota(tile_no[:, :, :], [[1, ET], [0, E]], base=0, channel_multiplier=0,
                      allow_small_or_imprecise_dtypes=True).then_inc(cst, 1)
            pool.wait_ge(cst, 15)
            pool.iota(filler[:, 2 * D:2 * D + 1], [[0, 1]], base=B * T, channel_multiplier=1,
                      allow_small_or_imprecise_dtypes=True).then_inc(cst, 1)
            pool.wait_ge(cst, 16)

            def norm_power(t, k):
                stat_ok.wait(pool, t, 3)
                pool.tensor_tensor(inv_std[:, k:k + 1], var_eps[:, k:k + 1], minus_half[:, :],
                                   ALU.pow).then_inc(inv_ok.sem, 1)

            PIECE = MATS * KC * F // (NT // RING4)
            raw_flat = raw[:, :, :, :].rearrange("p m c f -> p (m c f)")
            hi_flat = w_hi[:, 0, :, :, :].rearrange("p m c f -> p (m c f)")
            lo_flat = w_lo[:, 0, :, :, :].rearrange("p m c f -> p (m c f)")

            def piece(i):
                cols = bass.ds(i * PIECE, PIECE)
                pool.tensor_copy(hi_flat[:, cols], raw_flat[:, cols]).then_inc(e_hi, 1)
                pool.wait_ge(e_hi, i + 1)
                pool.tensor_tensor(lo_flat[:, cols], raw_flat[:, cols], hi_flat[:, cols].bitcast(F32),
                                   ALU.subtract).then_inc(e_lo, 1)

            def shared_step(t, k, first, last):
                route.wait(pool, t, 6)
                pool.tensor_tensor(exp_minus[:, :], euler[:, :], minus_top[:, :], ALU.pow).then_inc(exp_ok.sem, 1)
                if k == 2:
                    if isinstance(t, int) and t < RING4:
                        pool.wait_ge(raw_in, 16 * 2 * MATS)
                    piece((t - 2) // RING4 if isinstance(t, int) else it[0])
                if not last and not (isinstance(t, int) and t + 2 >= NT):
                    norm_power(t + 2, (k + 2) % RING4)
                if not first:
                    scatter(t - 1, (k - 1) % RING4)

            def scatter(t, k):
                placed.wait(pool, t, 5)
                xs_ok.wait(pool, t, 2)
                y_ok.wait(pool, t, 1)
                carried.wait(pool, t, 1 - RING4)
                pool.tensor_tensor(mark_p[:, k:k + 1], euler[:, :], euler[:, :], ALU.add).then_inc(carried.sem, 1)
                pool.indirect_dma_start(out=rows, out_offset=bass.IndirectOffsetOnAxis(ap=target[:, k:k + 1], axis=0),
                                        in_=row[:, k, :], in_offset=None).then_inc(row_io[k].sem, 16)

            norm_power(0, 0)
            norm_power(1, 1)
            it = [None]
            for k in range(RING4):
                shared_step(k, k, k == 0, False)
            with pool.Fori(1, NT // RING4 - 1) as i:
                it[0] = i
                for k in range(RING4):
                    shared_step(i * RING4 + k, k, False, False)
            for k in range(RING4):
                shared_step(NT - RING4 + k, k, False, k == RING4 - 1)
            scatter(NT - 1, RING4 - 1)
            pool.wait_ge(e_lo, NT // RING4)
            for m, w in enumerate((w_gate, w_up, w_down)):
                pool.dma_start(raw[:, m, :, :], w[1, :, :].rearrange("(c p) n -> p c n", p=P)).then_inc(fetched, 16)
            pool.wait_ge(fill_ok, 1)
            for k in range(RING4):
                pool.wait_ge(row_io[k].sem, 16 * (NT // RING4))
            for e in range(E):
                pool.indirect_dma_start(out=rows, out_offset=bass.IndirectOffsetOnAxis(ap=fill_row[:, e:e + 1], axis=0),
                                        in_=filler[:, :], in_offset=None).then_inc(fill_io, 16)
            pool.dma_start(rows[NULL_ROW:NULL_ROW + P, :], filler[:, :]).then_inc(fill_io, 16)
            pool.wait_ge(table_ok, 1)

            def expert_step(t, k, first, last):
                j = t - NT
                new = pool.value_load(tab[0:1, FIRST, bass.ds(j, 1)], min_val=0, max_val=1)
                e = pool.value_load(tab[0:1, EID, bass.ds(j, 1)], min_val=0, max_val=E - 1)
                with pool.If(new > 0):
                    odd = pool.value_load(tab[0:1, ODD, bass.ds(j, 1)], min_val=0, max_val=1)
                    pool.wait_ge(y_full.sem, t)
                    pool.wait_ge(fetched, (e + 1) * 16 * MATS)
                    for m in range(MATS):
                        hi = w_hi[:, bass.ds(1 - odd, 1), m, :, :].rearrange("p o c f -> p (o c f)")
                        lo = w_lo[:, bass.ds(1 - odd, 1), m, :, :].rearrange("p o c f -> p (o c f)")
                        src = raw[:, m, :, :].rearrange("p c f -> p (c f)")
                        if m == 0:
                            pool.tensor_tensor(mark_p[:, RING4:RING4 + 1], euler[:, :], euler[:, :], ALU.add)
                        pool.tensor_copy(hi, src).then_inc(e_hi, 1)
                        pool.wait_ge(e_hi, NT // RING4 + e * MATS + m + 1)
                        pool.tensor_tensor(lo, src, hi.bitcast(F32), ALU.subtract).then_inc(e_lo, 1)
                    pool.wait_ge(e_lo, NT // RING4 + (e + 1) * MATS)
                    pool.tensor_tensor(mark_p[:, RING4 + 1:], euler[:, :], euler[:, :], ALU.add)
                    nxt = pool.value_load(tab[0:1, FETCH, bass.ds(j, 1)], min_val=0, max_val=E - 1)
                    for m, w in enumerate((w_gate, w_up, w_down)):
                        pool.dma_start(raw[:, m, :, :], w[bass.ds(nxt, 1), :, :]
                                       .rearrange("o (c p) n -> p (o c) n", p=P)).then_inc(fetched, 16)
                if not first:
                    deliver(t - 1, (k - 1) % RING4)

            def deliver(t, k):
                y_ok.wait(pool, t, 1)
                carried.wait(pool, t, 1 - RING4)
                pool.tensor_tensor(mark_p[:, k:k + 1], euler[:, :], euler[:, :], ALU.add).then_inc(carried.sem, 1)
                pool.indirect_dma_start(out=out, out_offset=bass.IndirectOffsetOnAxis(ap=target[:, k:k + 1], axis=0),
                                        in_=y_out[:, k, :], in_offset=None, bounds_check=B * T - 1,
                                        oob_is_err=False).then_inc(y_io[k].sem, 16)

            tiles(pool, NT, ET, expert_step)
            deliver(NT + ET - 1, RING4 - 1)
            for k in range(RING4):
                pool.wait_ge(y_io[k].sem, 16 * (ET // RING4))
            pool.wait_ge(fetched, 16 * MATS * E)

        @block.scalar
        def _(act):
            def copy(out_, in_):
                return act.activation(out_, in_, ACT.Copy)

            for m in range(MATS):
                act.wait_ge(raw_in, 16 * MATS)
                copy(w_hi[:, 1, m, :, :], raw[:, m, :, :]).then_inc(sh_hi, 1)
            act.wait_ge(wr_in, 16)
            copy(wr_hi[:, :, :], wr[:, :, :]).then_inc(wr_ok, 1)

            def high_x(t):
                x_full.wait(act, t, 1)
                copy(x_hi[:, :, :], ps_xt[:, :].rearrange("p (c t) -> p c t", t=P)).then_inc(xhi_ok.sem, 1)

            def high_h(t):
                h_full.wait(act, t, 1)
                y_full.wait(act, t, 0)
                copy(h_hi[:, :, :], ps_ht[:, :].rearrange("p (c t) -> p c t", t=P)).then_inc(hhi_ok.sem, 1)

            def step(t, k, first, last):
                g_full.wait(act, t, 1)
                hid_ok.wait(act, t, 0)
                act.activation(silu[:, :], ps_g[:, :], ACT.Silu).then_inc(silu_ok.sem, 1)
                if not first:
                    high_h(t - 1)
                if not last:
                    high_x(t + 1)

            for t0, n in ((0, NT), (NT, ET)):
                high_x(t0)
                tiles(act, t0, n, step)
                high_h(t0 + n - 1)

        @block.vector
        def _(dve):
            def minus(o, a, b):
                return dve.tensor_tensor(o, a, b.bitcast(F32), ALU.subtract)

            dve.memset(chosen_so_far[:, :], 0.0).then_inc(cst_v, 1)

            def stats_of(t, k):
                ring_dma(dve, xt_in, t, k, 1)
                dve.bn_stats(st[:, k, :], xt[:, k, :]).then_inc(stat_ok.sem, 1)
                stat_ok.wait(dve, t, 1)
                dve.memset(mark_v[:, :], 0.0)
                dve.bn_aggr(mean_var[:, k, :], st[:, k, :]).then_inc(stat_ok.sem, 1)
                stat_ok.wait(dve, t, 2)
                dve.tensor_scalar(var_eps[:, k:k + 1], mean_var[:, k, 1:2], EPS, None, ALU.add) \
                    .then_inc(stat_ok.sem, 1)

            def normalise(t, k):
                inv_ok.wait(dve, t, 1)
                dve.tensor_scalar(xn[:, k, :], xt[:, k, :], mean_var[:, k, 0:1], inv_std[:, k:k + 1],
                                  ALU.subtract, ALU.mult).then_inc(xn_ok.sem, 1)

            def low_x(t):
                xhi_ok.wait(dve, t, 1)
                minus(x_lo[:, :, :], ps_xt[:, :].rearrange("p (c t) -> p c t", t=P),
                      x_hi[:, :, :]).then_inc(xlo_ok.sem, 1)

            def low_h(t):
                hhi_ok.wait(dve, t, 1)
                minus(h_lo[:, :, :], ps_ht[:, :].rearrange("p (c t) -> p c t", t=P),
                      h_hi[:, :, :]).then_inc(hlo_ok.sem, 1)

            def hidden(t):
                silu_ok.wait(dve, t, 1)
                u_full.wait(dve, t, 1)
                h_full.wait(dve, t, 0)
                dve.tensor_tensor(hid[:, :], ps_u[:, :], silu[:, :], ALU.mult).then_inc(hid_ok.sem, 1)

            def choose(t):
                l_full.wait(dve, t, 1)
                dve.tensor_copy(logits[:, :], ps_l[:, 0:E]).then_inc(route.sem, 1)
                route.wait(dve, t, 1)
                dve.tensor_reduce(top[:, :], logits[:, :], AX.X, ALU.max).then_inc(route.sem, 1)
                route.wait(dve, t, 2)
                dve.scalar_tensor_tensor(rank_of[:, :], logits[:, :], top[:, 0:1], first_wins[:, :],
                                         ALU.is_equal, ALU.mult).then_inc(route.sem, 1)
                route.wait(dve, t, 3)
                dve.tensor_reduce(winner[:, :], rank_of[:, :], AX.X, ALU.max).then_inc(route.sem, 1)
                route.wait(dve, t, 4)
                placed.wait(dve, t, 0)
                dve.tensor_scalar(chosen[:, :], rank_of[:, :], winner[:, 0:1], None, ALU.is_equal) \
                    .then_inc(route.sem, 1)
                dve.tensor_scalar(minus_top[:, :], top[:, :], -1.0, None, ALU.mult).then_inc(route.sem, 1)

            def scale(t, k):
                exp_ok.wait(dve, t, 1)
                dve.tensor_scalar(denom[:, :], exp_minus[:, :], 1.0, None, ALU.add).then_inc(score_ok.sem, 1)
                score_ok.wait(dve, t, 1)
                dve.reciprocal(score[:, :], denom[:, :]).then_inc(score_ok.sem, 1)
                score_ok.wait(dve, t, 2)
                ring_dma(dve, row_io, t, k, 0)
                dve.tensor_scalar(row[:, k, 0:D], xn[:, k, :], score[:, 0:1], None, ALU.mult) \
                    .then_inc(xs_ok.sem, 1)
                token_ok.wait(dve, t, 0)
                dve.tensor_scalar(row[:, k, 2 * D:ROW], filler[:, 2 * D:ROW], 0.0, token[:, 0:1],
                                  ALU.mult, ALU.add).then_inc(xs_ok.sem, 1)

            def put(t, k):
                k_full.wait(dve, t, 1)
                dve.tensor_tensor(place[:, :], ps_k[:, 0:E], region[:, :], ALU.add).then_inc(placed.sem, 1)
                placed.wait(dve, t, 1)
                dve.tensor_tensor(place1[:, :], place[:, :], chosen[:, :], ALU.mult).then_inc(placed.sem, 1)
                placed.wait(dve, t, 2)
                dve.tensor_reduce(place_sum[:, :], place1[:, :], AX.X, ALU.add).then_inc(placed.sem, 1)
                placed.wait(dve, t, 3)
                ring_dma(dve, row_io, t, k, 0)
                dve.tensor_copy(target[:, k:k + 1], place_sum[:, :]).then_inc(placed.sem, 1)
                dve.tensor_tensor(chosen_so_far[:, :], chosen_so_far[:, :], chosen[:, :],
                                  ALU.add).then_inc(placed.sem, 1)

            def shared_out(t, k):
                y_full.wait(dve, t, 1)
                dve.tensor_tensor(row[:, k, D:2 * D], ps_y[:, :], xt[:, k, :], ALU.add).then_inc(y_ok.sem, 1)
                xs_ok.wait(dve, t, 2)
                dve.tensor_scalar(token[:, :], token[:, :], float(P), None, ALU.add).then_inc(token_ok.sem, 1)

            def shared_step(t, k, first, last):
                if not first:
                    low_h(t - 1)
                    put(t - 1, (k - 1) % RING4)
                hidden(t)
                choose(t)
                if not last:
                    low_x(t + 1)
                if not first:
                    shared_out(t - 1, (k - 1) % RING4)
                if not (isinstance(t, int) and t + 2 >= NT):
                    stats_of(t + 2, (k + 2) % RING4)
                scale(t, k)
                if not (isinstance(t, int) and t + 2 >= NT):
                    normalise(t + 2, (k + 2) % RING4)

            stats_of(0, 0)
            stats_of(1, 1)
            for m in range(MATS):
                dve.wait_ge(sh_hi, m + 1)
                minus(w_lo[:, 1, m, :, :], raw[:, m, :, :], w_hi[:, 1, m, :, :]).then_inc(sh_lo, 1)
            dve.wait_ge(wr_ok, 1)
            minus(wr_lo[:, :, :], wr[:, :, :], wr_hi[:, :, :]).then_inc(wr_ok, 1)
            dve.wait_ge(cst, 16)
            normalise(0, 0)
            normalise(1, 1)
            low_x(0)
            tiles(dve, 0, NT, shared_step)
            low_h(NT - 1)
            put(NT - 1, RING4 - 1)
            shared_out(NT - 1, RING4 - 1)

            n_table = [0]

            def link(ins):
                ins.then_inc(table, 1)
                n_table[0] += 1
                dve.wait_ge(table, n_table[0])

            dve.wait_ge(count_ps, 1)
            link(dve.tensor_copy(counts[:, :], ps_k[:, 0:E]))
            link(dve.tensor_tensor(fill_at[:, :], counts[:, :], region[:, :], ALU.add))
            link(dve.tensor_scalar(fill_at[:, :], fill_at[:, :], lane[:, 0:1], None, ALU.add))
            dve.tensor_copy(fill_row[:, :], fill_at[:, :]).then_inc(fill_ok, 1)
            link(dve.tensor_tensor(over[:, :, :], counts[:, :].rearrange("p (e o) -> p e o", o=1)
                                   .to_broadcast([P, E, NT]), steps128[:, :, :], ALU.is_gt))
            link(dve.tensor_reduce(tiles_of[:, :], over[:, :, :], AX.X, ALU.add))
            link(dve.tensor_scalar(tiles_of[:, :], tiles_of[:, :], 1.0, None, ALU.max))
            link(dve.tensor_scalar(jump[:, :], tiles_of[:, :], -float(P), float(REGION), ALU.mult, ALU.add))
            link(dve.tensor_copy(tile_end[:, :], tiles_of[:, :]))
            for e in range(1, E):
                link(dve.tensor_tensor(tile_end[:, e:e + 1], tile_end[:, e - 1:e], tile_end[:, e:e + 1], ALU.add))
            link(dve.tensor_tensor(passed[:, :, :], tile_no[:, :, :],
                                   tile_end[:, :].rearrange("p (o e) -> p o e", o=1).to_broadcast([P, ET, E]),
                                   ALU.is_ge))
            link(dve.tensor_tensor(weighted_p[:, :, :], passed[:, :, :],
                                   jump[:, :].rearrange("p (o e) -> p o e", o=1).to_broadcast([P, ET, E]),
                                   ALU.mult))
            link(dve.tensor_reduce(tabf[:, EID, :], passed[:, :, 0:E - 1], AX.X, ALU.add))
            link(dve.tensor_reduce(tabf[:, BASE, :], weighted_p[:, :, :], AX.X, ALU.add))
            link(dve.scalar_tensor_tensor(tabf[:, BASE, :], tile_no[:, :, 0], float(P), tabf[:, BASE, :],
                                          ALU.mult, ALU.add))
            link(dve.tensor_scalar(tabf[:, BASE, :], tabf[:, BASE, :], float(NULL_ROW), None, ALU.min))
            link(dve.tensor_reduce(tabf[:, TMP, :], passed[:, :, 1:E - 1:2], AX.X, ALU.add))
            link(dve.scalar_tensor_tensor(tabf[:, ODD, :], tabf[:, TMP, :], -2.0, tabf[:, EID, :],
                                          ALU.mult, ALU.add))
            link(dve.memset(tabf[:, FIRST, 0:1], 1.0))
            link(dve.tensor_tensor(tabf[:, FIRST, 1:ET], tabf[:, EID, 1:ET], tabf[:, EID, 0:ET - 1], ALU.subtract))
            link(dve.tensor_scalar(tabf[:, TMP, :], tabf[:, EID, :], float(E - 1), None, ALU.is_lt))
            link(dve.tensor_tensor(tabf[:, FIRST, :], tabf[:, FIRST, :], tabf[:, TMP, :], ALU.mult))
            link(dve.tensor_scalar(tabf[:, FETCH, :], tabf[:, EID, :], 2.0, float(E - 1), ALU.add, ALU.min))
            dve.tensor_copy(tab[:, :, :], tabf[:, 0:5, :]).then_inc(table_ok, 1)

            def expert_out(t, k):
                y_full.wait(dve, t, 1)
                ring_dma(dve, y_io, t - NT, k, 0)
                dve.tensor_copy(target[:, k:k + 1], row[:, k, 2 * D:2 * D + 1])
                dve.tensor_tensor(y_out[:, k, :], ps_y[:, :], row[:, k, D:2 * D], ALU.add).then_inc(y_ok.sem, 1)

            def expert_step(t, k, first, last):
                if not first:
                    low_h(t - 1)
                hidden(t)
                if not last:
                    low_x(t + 1)
                if not first:
                    expert_out(t - 1, (k - 1) % RING4)

            low_x(NT)
            tiles(dve, NT, ET, expert_step)
            low_h(NT + ET - 1)
            expert_out(NT + ET - 1, RING4 - 1)

        @block.tensor
        def _(pe):
            pe.wait_ge(cst, 16)
            pe.wait_ge(cst_v, 1)

            def weights(m, c, s):
                if isinstance(s, int):
                    return w_hi[:, s, m, c, :], w_lo[:, s, m, c, :]
                at = bass.ds(s, 1)
                return (w_hi[:, at, m, c, :].rearrange("p o f -> p (o f)"),
                        w_lo[:, at, m, c, :].rearrange("p o f -> p (o f)"))

            def transpose_x(t, k):
                xlo_ok.wait(pe, t, 0)
                if shared[0]:
                    xn_ok.wait(pe, t, 1)
                    src = xn
                else:
                    ring_dma(pe, row_in, t - NT, k, 1)
                    src = row
                for c in range(KC):
                    last = pe.transpose(ps_xt[:, c * P:(c + 1) * P], src[:, k, c * P:(c + 1) * P], identity[:, :])
                last.then_inc(x_full.sem, 1)

            def gate(t, s):
                xlo_ok.wait(pe, t, 1)
                silu_ok.wait(pe, t, 0)
                products(pe, ps_g[:, :], [((x_hi[:, c, :], x_lo[:, c, :]), weights(0, c, s))
                                          for c in range(KC)]).then_inc(g_full.sem, 1)

            def up(t, s):
                hid_ok.wait(pe, t, 0)
                products(pe, ps_u[:, :], [((x_hi[:, c, :], x_lo[:, c, :]), weights(1, c, s))
                                          for c in range(KC)]).then_inc(u_full.sem, 1)

            def transpose_h(t):
                hid_ok.wait(pe, t, 1)
                hlo_ok.wait(pe, t, 0)
                for c in range(KC):
                    last = pe.transpose(ps_ht[:, c * P:(c + 1) * P], hid[:, c * P:(c + 1) * P], identity[:, :])
                last.then_inc(h_full.sem, 1)

            def down(t, s):
                hlo_ok.wait(pe, t, 1)
                y_ok.wait(pe, t, 0)
                products(pe, ps_y[:, :], [((h_hi[:, c, :], h_lo[:, c, :]), weights(2, c, s))
                                          for c in range(KC)]).then_inc(y_full.sem, 1)

            def router(t):
                route.wait(pe, t, -5)
                products(pe, ps_l[:, 0:E], [((x_hi[:, c, :], x_lo[:, c, :]), (wr_hi[:, c, :], wr_lo[:, c, :]))
                                            for c in range(KC)]).then_inc(l_full.sem, 1)

            def ranks(t):
                route.wait(pe, t, 5)
                placed.wait(pe, t, 0)
                pe.matmul(ps_k[:, 0:E], before[:, :], chosen[:, :], start=True, stop=False)
                pe.matmul(ps_k[:, 0:E], all_ones[:, :], chosen_so_far[:, :], start=False,
                          stop=True).then_inc(k_full.sem, 1)

            def shared_step(t, k, first, last):
                gate(t, 1)
                if not first:
                    ranks(t - 1)
                    transpose_h(t - 1)
                up(t, 1)
                router(t)
                if not last:
                    transpose_x(t + 1, (k + 1) % RING4)
                if not first:
                    down(t - 1, 1)

            shared = [True]
            pe.wait_ge(sh_lo, MATS)
            pe.wait_ge(wr_ok, 2)
            transpose_x(0, 0)
            tiles(pe, 0, NT, shared_step)
            ranks(NT - 1)
            transpose_h(NT - 1)
            down(NT - 1, 1)
            placed.wait(pe, NT, 0)
            pe.matmul(ps_k[:, 0:E], all_ones[:, :], chosen_so_far[:, :], start=True, stop=True).then_inc(count_ps, 1)
            pe.wait_ge(table_ok, 1)

            def expert_step(t, k, first, last):
                j = t - NT
                e = pe.value_load(tab[0:1, EID, bass.ds(j, 1)], min_val=0, max_val=E - 1)
                s = pe.value_load(tab[0:1, ODD, bass.ds(j, 1)], min_val=0, max_val=1)
                pe.wait_ge(e_lo, NT // RING4 + e * MATS)
                gate(t, s)
                if not first:
                    transpose_h(t - 1)
                up(t, s)
                if not last:
                    transpose_x(t + 1, (k + 1) % RING4)
                if not first:
                    s0 = pe.value_load(tab[0:1, ODD, bass.ds(j - 1, 1)], min_val=0, max_val=1)
                    down(t - 1, s0)

            shared[0] = False
            transpose_x(NT, 0)
            tiles(pe, NT, ET, expert_step)
            transpose_h(NT + ET - 1)
            s = pe.value_load(tab[0:1, ODD, ET - 1:ET], min_val=0, max_val=1)
            down(NT + ET - 1, s)


_INS = ['L0_attn_x', 'L0_attn_w_attn', 'L0_attn_w_out', 'L0_ffn_router_w', 'L0_ffn_gate_w', 'L0_ffn_up_w',
        'L0_ffn_down_w', 'L0_ffn_shared_gate_w', 'L0_ffn_shared_up_w', 'L0_ffn_shared_down_w']


def kernel(**inputs):
    import numpy as _np
    import concourse.bacc as _bacc
    from concourse.bass_utils import run_bass_kernel_spmd as _run

    nc = _bacc.Bacc("TRN2", target_bir_lowering=False, num_devices=1)
    arrays, args = {}, []
    for name in _INS:
        a = _np.ascontiguousarray(inputs[name])
        arrays[f"in_{name}_dram"] = a
        args.append(nc.dram_tensor(f"in_{name}_dram", a.shape, mybir.dt.from_np(a.dtype), kind="ExternalInput").ap())
    arrays["rope"] = rope_table()
    rope = nc.dram_tensor("rope", arrays["rope"].shape, F32, kind="ExternalInput").ap()
    q_dram = nc.dram_tensor("q_dram", (B, G, 2, P, T), F32, kind="Internal").ap()
    x1 = nc.dram_tensor("x1_dram", (B * T, D), F32, kind="Internal").ap()
    rows = nc.dram_tensor("rows_dram", (SORTED_ROWS, ROW), F32, kind="Internal").ap()
    out = nc.dram_tensor("out_0_dram", (B * T, D), F32, kind="ExternalOutput").ap()
    x, w_attn, w_out, *ffn = args
    attention(nc, x, w_attn, w_out, rope, q_dram, x1)
    experts(nc, x1, *ffn, rows, out)
    r = _run(nc, [arrays], core_ids=[0])
    return r.results[0]["out_0_dram"].reshape(B, T, D)
```

```python
import concourse.bass as bass
from concourse import mybir
from contextlib import ExitStack, contextmanager

F32 = mybir.dt.float32
F32R = mybir.dt.float32r
BF16 = mybir.dt.bfloat16
I32 = mybir.dt.int32
U32 = mybir.dt.uint32
ALU = mybir.AluOpType
ACT = mybir.ActivationFunctionType
AX = mybir.AxisListType

P = 128
B, T, D = 8, 512, 512
H, HD = 16, 32
KC = D // P
TT = T // P
GH = P // HD
G = H // GH
NQ = 1 + G
QKV = NQ * P
SCALE = HD ** -0.5
EPS = 1e-5
SROWS = 3 * HD + 1
HALF_SWAP = [(i + HD // 2) % HD for i in range(HD)]


def static_zero(b):
    return isinstance(b, int) and b == 0


class Counter:

    def __init__(self, sem, per):
        self.sem, self.per = sem, per

    def wait(self, eng, b, k):
        v = b * self.per + k
        if not isinstance(v, int) or v > 0:
            eng.wait_ge(self.sem, v)


RING = 3
C_FIRST = 2
USES = {"C": range(C_FIRST, C_FIRST + TT), "T": range(H * KC)}
PER_BANK = {s: [sum(u % RING == k for u in r) for k in range(RING)] for s, r in USES.items()}
A_USES = KC + NQ
OUT_TERMS = 3 * G


def out_plan():
    order = [(t, i) for t in range(2) for i in range(OUT_TERMS - 3)] + \
            [(t, i) for t in range(2) for i in range(OUT_TERMS - 3, OUT_TERMS)] + \
            [(t, i) for t in range(2, TT) for i in range(OUT_TERMS)]
    plan = {1: order[:OUT_TERMS - 3]}
    rest, tiles = order[OUT_TERMS - 3:], range(2, 2 * GH * TT)
    for k, n in enumerate(tiles):
        plan[n] = rest[k * len(rest) // len(tiles):(k + 1) * len(rest) // len(tiles)]
    return plan


OUT_PLAN = out_plan()
RESIDUAL_AT = {n + 1: t for n, plan in OUT_PLAN.items() for t, i in plan if i == OUT_TERMS - 1}
SUMS_AT = {1: ((0, 1), (0, 2)), 2: ((0, 3), (1, 0)), 3: ((0, 3), (1, 0))}


def ring_bank(stage, u):
    return USES[stage][u] % RING


def ring_count(stage, b, u, bank=None):
    k = ring_bank(stage, u) if bank is None else bank
    here = sum(v % RING == k for v in USES[stage][:u + 1])
    if stage == "C":
        return (b + 1) * PER_BANK["T"][k] + b * PER_BANK["C"][k] + here
    return b * (PER_BANK["T"][k] + PER_BANK["C"][k]) + here


def ring_wait(eng, sems, stage, b, u):
    eng.wait_ge(sems[ring_bank(stage, u)], ring_count(stage, b, u))


def ring_take(eng, free, stage, b, u):
    n = ring_count(stage, b, u) - 1
    if not isinstance(n, int) or n > 0:
        eng.wait_ge(free[ring_bank(stage, u)], n)


def ring_wait_all(eng, sems, stage, b, u):
    for k in range(RING):
        eng.wait_ge(sems[k], ring_count(stage, b, u, k))


def terms(pairs):
    two = [term for (a, l), (c, m) in pairs for term in ((a, c), (l, c), (a, m))]
    return [(a, c, n == 0, n == len(two) - 1) for n, (a, c) in enumerate(two)]


def products(pe, out, pairs):
    for a, c, start, stop in terms(pairs):
        last = pe.matmul(out, a, c, start=start, stop=stop)
    return last


def attention(nc, x, w_attn, w_out, rope, q_dram, x1):
    with ExitStack() as ctx:
        def sb(name, shape, dt=F32):
            return ctx.enter_context(nc.sbuf_tensor(name, shape, dt))

        def sem(name):
            return ctx.enter_context(nc.semaphore(name))

        wq_hi = sb("wq_hi", [P, KC, QKV], F32R)
        wq_lo = sb("wq_lo", [P, KC, QKV], F32R)
        wo_hi = sb("wo_hi", [P, KC, D], F32R)
        wo_lo = sb("wo_lo", [P, KC, D], F32R)
        cos_sin = sb("cos_sin", [P, 2, T])
        ident = sb("ident", [P, P])
        ones = sb("ones", [P, HD])
        exponent = sb("exponent", [P, TT])
        xa = sb("xa", [P, TT, D])
        xT_hi = sb("xT_hi", [P, KC, T], F32R)
        xT_lo = sb("xT_lo", [P, KC, T], F32R)
        stats = sb("stats", [P, TT, 6])
        mv = sb("mv", [P, TT, 2])
        vareps = sb("vareps", [P, TT])
        rstd = sb("rstd", [P, TT])
        nbias = sb("nbias", [P, TT])
        q_raw = sb("q_raw", [P, T])
        q_rot = sb("q_rot", [P, 2, T])
        q_swap = sb("q_swap", [P, T])
        q_hi = sb("q_hi", [P, 2, T], F32R)
        q_lo = sb("q_lo", [P, 2, T], F32R)
        q_stack = sb("q_stack", [SROWS, H, T], F32R)
        k_stack = sb("k_stack", [SROWS, T], F32R)
        val = sb("val", [P, TT, HD])
        maxes = sb("maxes", [P, H * TT])
        neg_max = q_raw[0:GH * TT, 0:P].bitcast(F32R)
        probs = sb("probs", [P, 2 * GH, KC, T])
        psums = sb("psums", [P, GH, 2, T])
        mark = sb("mark", [P, 1])
        o_all = sb("o_all", [P, G, T])
        xres = sb("xres", [P, 2, D])

        ps_s = ctx.enter_context(nc.psum_tensor("ps_s", [P, 2, T], F32))
        ps_ring = ctx.enter_context(nc.psum_tensor("ps_ring", [P, RING, 512], F32))
        ps_o = ctx.enter_context(nc.psum_tensor("ps_o", [P, T], F32))
        ps_sum = ctx.enter_context(nc.psum_tensor("ps_sum", [P, T], F32))
        ps_x = ctx.enter_context(nc.psum_tensor("ps_x", [P, 512], F32))

        RAW = (H + 2) * HD
        raw_q = probs[:, 0:2 * GH, :, :].rearrange("p h c t -> p (h c t)")[:, 0:KC * RAW] \
            .rearrange("p (c n) -> p c n", c=KC)
        raw_o = probs[:, 0:2 * GH, :, :].rearrange("p h c t -> p (h c t)")[:, GH * KC * T:GH * KC * T + KC * D] \
            .rearrange("p (c n) -> p c n", c=KC)

        raw_q_in, raw_o_in, rope_in = sem("raw_q_in"), sem("raw_o_in"), sem("rope_in")
        const_ok, ones_ok = sem("const_ok"), sem("ones_ok")
        w_hi_ok, w_lo_ok = sem("w_hi_ok"), sem("w_lo_ok")
        x_in = Counter(sem("x_in"), 16)
        ln_stats = Counter(sem("ln_stats"), 2 * TT + 1)
        ln_rstd = Counter(sem("ln_rstd"), 1)
        ln_bias = Counter(sem("ln_bias"), 1)
        ln_done = Counter(sem("ln_done"), TT)
        a_full = Counter(sem("a_full"), A_USES)
        a_free = Counter(sem("a_free"), A_USES)
        full = [sem(f"ring_full{k}") for k in range(RING)]
        free = [sem(f"ring_free{k}") for k in range(RING)]
        xt_hi = Counter(sem("xt_hi"), KC)
        raw_ok = Counter(sem("raw_ok"), NQ)
        swap_ok = Counter(sem("swap_ok"), NQ)
        sin_ok = Counter(sem("sin_ok"), NQ)
        rot_ok = Counter(sem("rot_ok"), NQ)
        hi_ok = Counter(sem("hi_ok"), NQ)
        k_ok = Counter(sem("k_ok"), 1)
        lo_ok = Counter(sem("lo_ok"), NQ)
        q_out = [Counter(sem(f"q_out{k}"), 32 * (G // 2)) for k in range(2)]
        q_in = [Counter(sem(f"q_in{g}"), 16 * 3) for g in range(G)]
        x_full = Counter(sem("x_full"), 1 + G)
        x_free = Counter(sem("x_free"), 1 + G)
        s_full = Counter(sem("s_full"), H * TT)
        s_free = Counter(sem("s_free"), H * TT)
        shift_in = Counter(sem("shift_in"), 16 * G)
        pair_ok = Counter(sem("pair_ok"), 2 * H)
        pv_done = Counter(sem("pv_done"), G * KC)
        sum_done = Counter(sem("sum_done"), G)
        rec_ok = Counter(sem("rec_ok"), G * TT)
        o_ok = Counter(sem("o_ok"), G)
        oT_hi = Counter(sem("oT_hi"), G)
        oT_lo = Counter(sem("oT_lo"), G)
        xr_in = [Counter(sem(f"xr_in{k}"), 16 * TT // 2) for k in range(2)]
        x1_out = [Counter(sem(f"x1_out{k}"), 16 * TT // 2) for k in range(2)]

        block = ctx.enter_context(nc.Block())

        def batches(eng, batch):
            batch(0, True, False, True)
            with eng.Fori(1, B - 2) as b:
                batch(b, False, False, True)
            batch(B - 2, False, False, False)
            batch(B - 1, False, True, False)

        KV = NQ - 1
        XT_SLOT = 2 * GH
        def projected(s):
            return s - (XT_SLOT + 2)

        def slot_stored(eng, b, p):
            q_out[p % 2].wait(eng, b, 32 * (p // 2))

        @block.sync
        def _(sp):
            def load_x(b):
                a_full.wait(sp, b - 1, KC)
                sp.dma_start(xa[:, :, :], x[bass.ds(b, 1), :, :].rearrange("b (t p) d -> p (b t) d", p=P)) \
                    .then_inc(x_in.sem, 16)

            def load_residual(b, t):
                x1_out[t % 2].wait(sp, b, 16 * (t // 2))
                sp.dma_start(xres[:, t % 2, :], x[bass.ds(b, 1), t * P:(t + 1) * P, :]
                             .rearrange("b p d -> (b p) d")).then_inc(xr_in[t % 2].sem, 16)

            def store_x1(b, t):
                ring_wait(sp, free, "C", b, t)
                sp.dma_start(x1[bass.ds(b * T + t * P, P), :],
                             xres[:, t % 2, :]).then_inc(x1_out[t % 2].sem, 16)
                if t + 2 < TT:
                    load_residual(b, t + 2)

            def stack(b, g):
                for part, ok, i in ((q_hi, hi_ok, 0), (q_lo, lo_ok, 1)):
                    ok.wait(sp, b, g + 1)
                    sp.dma_start(q_dram[bass.ds(b, 1), g, i, :, :].rearrange("b p t -> (b p) t"),
                                 part[:, g % 2, :].bitcast(F32)).then_inc(q_out[g % 2].sem, 16)
                q_out[g % 2].wait(sp, b, 32 * (g // 2 + 1))
                for r, i in enumerate((0, 1, 0)):
                    sp.dma_start(q_stack[r * HD:(r + 1) * HD, g * GH:(g + 1) * GH, :].bitcast(F32),
                                 q_dram[bass.ds(b, 1), g, i, :, :]
                                 .rearrange("b (j d) t -> d (b j) t", j=GH)).then_inc(q_in[g].sem, 16)

            def shift(b, g):
                x_free.wait(sp, b, 1 + g + 1)
                sp.dma_start(q_stack[SROWS - 1:SROWS, g * GH:(g + 1) * GH, :].bitcast(F32),
                             neg_max.bitcast(F32)).then_inc(shift_in.sem, 16)

            def batch(b, first, last, ahead):
                if not first:
                    load_residual(b - 1, 0)
                    load_residual(b - 1, 1)
                    store_x1(b - 1, 0)
                    store_x1(b - 1, 1)
                shift(b, 0)
                if not first:
                    store_x1(b - 1, 2)
                    store_x1(b - 1, 3)
                for g in range(1, G):
                    shift(b, g)
                if ahead:
                    load_x(b + 2)
                if not last:
                    for g in range(G):
                        stack(b + 1, g)

            sp.dma_start(raw_q, w_attn.rearrange("(c p) n -> p c n", p=P)).then_inc(raw_q_in, 16)
            sp.dma_start(xa[:, :, :], x[0, :, :].rearrange("(t p) d -> p t d", p=P)).then_inc(x_in.sem, 16)
            sp.dma_start(cos_sin[:, :, :], rope).then_inc(rope_in, 16)
            sp.dma_start(raw_o, w_out.rearrange("(c p) n -> p c n", p=P)).then_inc(raw_o_in, 16)
            load_x(1)
            for g in range(G):
                stack(0, g)
            batches(sp, batch)
            load_residual(B - 1, 0)
            load_residual(B - 1, 1)
            for t in range(TT):
                store_x1(B - 1, t)
            for k in range(2):
                x1_out[k].wait(sp, B, 0)

        @block.gpsimd
        def _(pool):
            pool.memset(ident[:, :], 0.0).then_inc(const_ok, 1)
            pool.wait_ge(const_ok, 1)
            pool.affine_select(out=ident[:, :], in_=ident[:, :], compare_op=ALU.not_equal, fill=1.0,
                               base=0, pattern=[[-1, P]], channel_multiplier=1).then_inc(const_ok, 1)
            pool.memset(ones[:, :], 1.0).then_inc(const_ok, 1)
            pool.memset(exponent[:, :], -0.5).then_inc(const_ok, 1)

            def rstd_of(b):
                ln_stats.wait(pool, b, 2 * TT + 1)
                ln_done.wait(pool, b, 0)
                pool.tensor_tensor(rstd[:, :], vareps[:, :], exponent[:, :], ALU.pow).then_inc(ln_rstd.sem, 1)

            def sines(b, p):
                swap_ok.wait(pool, b, p + 1)
                pool.tensor_tensor(q_swap[:, :], q_swap[:, :], cos_sin[:, 1, :],
                                   ALU.mult).then_inc(sin_ok.sem, 1)

            def add_pairs(b, h):
                slot, j = h % (2 * GH), h % GH
                sum_done.wait(pool, b, h // GH)
                for k in range(2):
                    ring_wait_all(pool, free, "T", b, h * KC + 2 * k + 1)
                    pool.tensor_tensor(psums[:, j, k, :], probs[:, slot, 2 * k, :], probs[:, slot, 2 * k + 1, :],
                                       ALU.add).then_inc(pair_ok.sem, 1)

            def output(b):
                for g in range(G):
                    oT_hi.wait(pool, b, g + 1)
                    pool.tensor_tensor(xT_lo[:, g, :], o_all[:, g, :], xT_hi[:, g, :].bitcast(F32),
                                       ALU.subtract).then_inc(oT_lo.sem, 1)

            def batch(b, first, last, ahead):
                if not first:
                    output(b - 1)
                if not last:
                    rstd_of(b + 1)
                for s in range(H):
                    p = projected(s - 1)
                    if 0 <= p < NQ and not last:
                        sines(b + 1, p)
                    add_pairs(b, s)

            pool.wait_ge(const_ok, 4)
            rstd_of(0)
            pool.wait_ge(rope_in, 16)
            for p in range(NQ):
                sines(0, p)
            batches(pool, batch)
            output(B - 1)

        @block.scalar
        def _(act):
            def copy(out, in_, scale=1.0):
                return act.activation(out, in_, ACT.Copy, scale=scale)

            def normalise(b, t):
                if t == 0:
                    ln_bias.wait(act, b, 1)
                act.activation(xa[:, t, :], xa[:, t, :], ACT.Identity, bias=nbias[:, t:t + 1],
                               scale=rstd[:, t:t + 1]).then_inc(ln_done.sem, 1)

            for t in range(TT):
                normalise(0, t)
            act.wait_ge(raw_q_in, 16)
            copy(wq_hi[:, :, 0:D], raw_q[:, :, 0:D]).then_inc(w_hi_ok, 1)
            for r in range(3):
                copy(wq_hi[:, :, D + r * HD:D + (r + 1) * HD], raw_q[:, :, D:D + HD]).then_inc(w_hi_ok, 1)
            copy(wq_hi[:, :, D + 3 * HD:QKV], raw_q[:, :, D + HD:D + 2 * HD]).then_inc(w_hi_ok, 1)
            act.wait_ge(raw_o_in, 16)
            copy(wo_hi[:, :, :], raw_o).then_inc(w_hi_ok, 1)

            def transposed(b, c):
                a_full.wait(act, b, c + 1)
                copy(xT_hi[:, c, :], ps_s[:, c % 2, :]).then_inc(xt_hi.sem, 1)

            def raw(b, p):
                a_full.wait(act, b, KC + p + 1)
                if p == 0:
                    shift_in.wait(act, b, 0)
                swap_ok.wait(act, b, p)
                copy(q_raw[:, :], ps_s[:, (KC + p) % 2, :]).then_inc(raw_ok.sem, 1)

            def high(b, p, first):
                rot_ok.wait(act, b, p + 1)
                slot_stored(act, b, p)
                lo_ok.wait(act, b, max(0, p - 1))
                if not first:
                    ring_wait(act, full, "T", b - 1, min((p + 1) * GH, H) * KC - 1)
                if p == KV:
                    copy(k_stack[0:2 * HD, :], q_rot[0:2 * HD, p % 2, :]).then_inc(k_ok.sem, 1)
                    copy(q_hi[2 * HD:3 * HD, p % 2, :], q_rot[2 * HD:3 * HD, p % 2, :]).then_inc(hi_ok.sem, 1)
                else:
                    copy(q_hi[:, p % 2, :], q_rot[:, p % 2, :]).then_inc(hi_ok.sem, 1)

            def output(b, g, last):
                if g == 0 and not last:
                    a_full.wait(act, b + 1, A_USES)
                o_ok.wait(act, b, g + 1)
                copy(xT_hi[:, g, :], o_all[:, g, :]).then_inc(oT_hi.sem, 1)

            def values(b):
                x_full.wait(act, b, 1)
                pv_done.wait(act, b, 0)
                copy(val[:, :, :], ps_x[:, :].rearrange("p (t d) -> p t d", d=P)[:, :, 3 * HD:P]).then_inc(x_free.sem, 1)

            def shifts(b, g):
                x_full.wait(act, b, 1 + g + 1)
                shift_in.wait(act, b, 16 * g)
                copy(neg_max, ps_x[0:GH * TT, 0:P], scale=-1.0).then_inc(x_free.sem, 1)

            def exps(b, h, first, chunks):
                if not (first and h < 2 * GH) and h % GH == 0 and chunks[0] == 0:
                    pv_done.wait(act, b, (h // GH - 1) * KC)
                    pair_ok.wait(act, b, (h // GH - 1) * GH * 2)
                for c in chunks:
                    u = h * KC + c
                    ring_wait(act, full, "T", b, u)
                    act.activation(probs[:, h % (2 * GH), c, :], ps_ring[:, ring_bank("T", u), :], ACT.Exp,
                                   scale=SCALE).then_inc(free[ring_bank("T", u)], 1)

            def batch(b, first, last, ahead):
                if not last:
                    for t in range(TT):
                        normalise(b + 1, t)
                shifts(b, 0)
                for s in range(H + 1):
                    p = projected(s - 1)
                    if 0 <= p < NQ and not last:
                        raw(b + 1, p)
                    if s < H:
                        exps(b, s, first, (0, 1))
                    if s % GH == 0 and s // GH + 1 < G:
                        shifts(b, s // GH + 1)
                    if 0 <= p - 1 < NQ and not last:
                        high(b + 1, p - 1, False)
                    if s < H:
                        exps(b, s, first, (2, 3))
                    if XT_SLOT <= s < XT_SLOT + 2 and not last:
                        for k in range(2):
                            transposed(b + 1, 2 * (s - XT_SLOT) + k)
                for g in range(G - 1):
                    output(b, g, last)
                if not last:
                    values(b + 1)
                output(b, G - 1, last)

            act.wait_ge(w_lo_ok, 6)
            for c in range(KC):
                transposed(0, c)
            for p in range(NQ + 1):
                if p < NQ:
                    raw(0, p)
                if p >= 1:
                    high(0, p - 1, True)
            values(0)
            batches(act, batch)

        @block.vector
        def _(dve):
            def minus(out, a, b):
                return dve.tensor_tensor(out, a, b.bitcast(F32), ALU.subtract)

            def statistics(b, t):
                if t == 0:
                    x_in.wait(dve, b, 16)
                dve.bn_stats(stats[:, t, :], xa[:, t, :]).then_inc(ln_stats.sem, 1)

            def variances(b):
                ln_stats.wait(dve, b, TT)
                dve.memset(mark[:, :], 0.0)
                for t in range(TT):
                    dve.bn_aggr(mv[:, t, :], stats[:, t, :]).then_inc(ln_stats.sem, 1)
                ln_stats.wait(dve, b, 2 * TT)
                dve.tensor_scalar(vareps[:, :], mv[:, :, 1], EPS, None, ALU.add).then_inc(ln_stats.sem, 1)

            def normalise_bias(b):
                ln_rstd.wait(dve, b, 1)
                dve.scalar_tensor_tensor(nbias[:, :], mv[:, :, 0], -1.0, rstd[:, :], ALU.mult, ALU.mult) \
                    .then_inc(ln_bias.sem, 1)

            dve.memset(k_stack[SROWS - 1:SROWS, :].bitcast(F32), 1.0).then_inc(ones_ok, 1)
            for t in range(TT):
                statistics(0, t)
            variances(0)
            normalise_bias(0)
            dve.wait_ge(w_hi_ok, 6)
            minus(wq_lo[:, :, 0:D], raw_q[:, :, 0:D], wq_hi[:, :, 0:D]).then_inc(w_lo_ok, 1)
            for r in range(3):
                cols = slice(D + r * HD, D + (r + 1) * HD)
                minus(wq_lo[:, :, cols], raw_q[:, :, D:D + HD], wq_hi[:, :, cols]).then_inc(w_lo_ok, 1)
            minus(wq_lo[:, :, D + 3 * HD:QKV], raw_q[:, :, D + HD:D + 2 * HD],
                  wq_hi[:, :, D + 3 * HD:QKV]).then_inc(w_lo_ok, 1)
            minus(wo_lo[:, :, :], raw_o, wo_hi[:, :, :]).then_inc(w_lo_ok, 1)
            dve.wait_ge(rope_in, 16)

            def transposed(b, c):
                xt_hi.wait(dve, b, c + 1)
                minus(xT_lo[:, c, :], ps_s[:, c % 2, :], xT_hi[:, c, :]).then_inc(a_free.sem, 1)

            def swap(b, p):
                rot_ok.wait(dve, b, p)
                raw_ok.wait(dve, b, p + 1)
                dve.tensor_tensor(q_rot[:, p % 2, :], ps_s[:, (KC + p) % 2, :], cos_sin[:, 0, :],
                                  ALU.mult).then_inc(a_free.sem, 1)
                dve.stream_shuffle(q_swap[:, :], q_raw[:, :], HALF_SWAP).then_inc(swap_ok.sem, 1)

            def rotate(b, p):
                a_free.wait(dve, b, KC + p + 1)
                sin_ok.wait(dve, b, p + 1)
                dve.tensor_tensor(q_rot[:, p % 2, :], q_rot[:, p % 2, :], q_swap[:, :],
                                  ALU.add).then_inc(rot_ok.sem, 1)

            def low(b, p):
                hi_ok.wait(dve, b, p + 1)
                if p == KV:
                    minus(k_stack[2 * HD:3 * HD, :], q_rot[2 * HD:3 * HD, p % 2, :],
                          q_hi[2 * HD:3 * HD, p % 2, :]).then_inc(lo_ok.sem, 1)
                else:
                    minus(q_lo[:, p % 2, :], q_rot[:, p % 2, :], q_hi[:, p % 2, :]).then_inc(lo_ok.sem, 1)

            def residual(b, t):
                xr_in[t % 2].wait(dve, b, 16 * (t // 2 + 1))
                ring_wait(dve, full, "C", b, t)
                dve.tensor_tensor(xres[:, t % 2, :], ps_ring[:, ring_bank("C", t), :], xres[:, t % 2, :],
                                  ALU.add).then_inc(free[ring_bank("C", t)], 1)

            def maximum(b, n):
                s_full.wait(dve, b, n + 1)
                dve.tensor_reduce(maxes[:, n:n + 1], ps_s[:, n % 2, :], AX.X, ALU.max).then_inc(s_free.sem, 1)

            def reciprocal(b, g, q):
                if q == 0:
                    oT_lo.wait(dve, b, 0)
                    sum_done.wait(dve, b, g + 1)
                cols = slice(q * P, (q + 1) * P)
                dve.reciprocal(o_all[:, g, cols], ps_sum[:, cols]).then_inc(rec_ok.sem, 1)

            def weigh(b, g):
                rec_ok.wait(dve, b, (g + 1) * TT)
                pv_done.wait(dve, b, (g + 1) * KC)
                dve.tensor_tensor(o_all[:, g, :], ps_o[:, :], o_all[:, g, :], ALU.mult).then_inc(o_ok.sem, 1)

            def batch(b, first, last, ahead):
                for n in range(2 * GH * TT):
                    maximum(b, n)
                    if n == GH * TT and not last:
                        normalise_bias(b + 1)
                    if not first and n in RESIDUAL_AT:
                        residual(b - 1, RESIDUAL_AT[n])
                for s in range(H + 1):
                    g, j, p = s // GH, s % GH, projected(s - 1)
                    for t in range(TT):
                        if g < 2:
                            maximum(b, ((g + 2) * GH + j) * TT + t)
                        if s == 0 and not first and 2 * GH * TT + t in RESIDUAL_AT:
                            residual(b - 1, RESIDUAL_AT[2 * GH * TT + t])
                    if 1 <= g < G and j == 2:
                        for k in range(2):
                            reciprocal(b, g - 1, 2 + k)
                    if 1 <= g < G and j == 3:
                        weigh(b, g - 1)
                    if 0 <= p - 1 < NQ and not last:
                        rotate(b + 1, p - 1)
                    if 0 <= p < NQ and not last:
                        swap(b + 1, p)
                    if XT_SLOT <= s < XT_SLOT + 2 and not last:
                        for k in range(2):
                            transposed(b + 1, 2 * (s - XT_SLOT) + k)
                    if 0 <= p - 1 < NQ and not last:
                        low(b + 1, p - 1)
                    if 1 <= g < G and j == 1:
                        for k in range(2):
                            reciprocal(b, g - 1, k)
                    if g == G - 1 and ahead:
                        statistics(b + 2, j)
                    if s == H:
                        if ahead:
                            variances(b + 2)
                        for k in range(TT):
                            reciprocal(b, G - 1, k)
                        weigh(b, G - 1)

            for c in range(KC):
                transposed(0, c)
            for p in range(NQ + 1):
                if p >= 1:
                    rotate(0, p - 1)
                if p < NQ:
                    swap(0, p)
                if p >= 1:
                    low(0, p - 1)
            for t in range(TT):
                statistics(1, t)
            variances(1)
            batches(dve, batch)
            for t in range(TT):
                residual(B - 1, t)

        @block.tensor
        def _(pe):
            pe.wait_ge(const_ok, 4)
            pe.wait_ge(ones_ok, 1)

            def take(b, u, first):
                if u >= 2:
                    a_free.wait(pe, b, u - 1)
                elif not first:
                    s_free.wait(pe, b, 0)

            def transposes(b, c, first):
                if c == 0:
                    ln_done.wait(pe, b, TT)
                take(b, c, first)
                for t in range(TT):
                    last = pe.transpose(ps_s[:, c % 2, t * P:(t + 1) * P],
                                        xa[:, t, c * P:(c + 1) * P], ident[:, :])
                last.then_inc(a_full.sem, 1)

            def projection(p):
                cols = slice(p * P, (p + 1) * P)
                return terms([((wq_hi[:, c, cols], wq_lo[:, c, cols]), (xT_hi[:, c, :], xT_lo[:, c, :]))
                              for c in range(KC)])

            def project(b, p, part, parts):
                if part == 0:
                    if p == 0:
                        a_free.wait(pe, b, KC)
                    take(b, KC + p, False)
                todo = projection(p)
                size = len(todo) // parts
                for a, c, start, stop in todo[part * size:(part + 1) * size]:
                    last = pe.matmul(ps_s[:, (KC + p) % 2, :], a, c, start=start, stop=stop)
                if part == parts - 1:
                    last.then_inc(a_full.sem, 1)

            def values(b):
                raw_ok.wait(pe, b, NQ)
                x_free.wait(pe, b, 0)
                for t in range(TT):
                    last = pe.transpose(ps_x[:, t * P:(t + 1) * P], q_raw[:, t * P:(t + 1) * P], ident[:, :])
                last.then_inc(x_full.sem, 1)

            def out_product(b, t, i):
                if i == 0:
                    ring_take(pe, free, "C", b, t)
                if t == 0 and i % 3 == 0:
                    oT_lo.wait(pe, b, i // 3 + 1)
                rows = slice(t * P, (t + 1) * P)
                a, c, start, stop = terms([((xT_hi[:, g, rows], xT_lo[:, g, rows]), (wo_hi[:, g, :], wo_lo[:, g, :]))
                                           for g in range(G)])[i]
                last = pe.matmul(ps_ring[:, ring_bank("C", t), :], a, c, start=start, stop=stop)
                if stop:
                    last.then_inc(full[ring_bank("C", t)], 1)

            def scores(b, n):
                h, t = n // TT, n % TT
                if n % (GH * TT) == 0:
                    q_in[h // GH].wait(pe, b, 16 * 3)
                if n == 0:
                    k_ok.wait(pe, b, 1)
                    lo_ok.wait(pe, b, NQ)
                if n < 2:
                    a_free.wait(pe, b, A_USES)
                else:
                    s_free.wait(pe, b, n - 1)
                pe.matmul(ps_s[:, n % 2, :], q_stack[0:3 * HD, h, t * P:(t + 1) * P],
                          k_stack[0:3 * HD, :], start=True, stop=True).then_inc(s_full.sem, 1)

            def max_rows(b, g):
                s_free.wait(pe, b, (g + 1) * GH * TT)
                x_free.wait(pe, b, 1 + g)
                cols = slice(g * GH * TT, (g + 1) * GH * TT)
                pe.transpose(ps_x[0:GH * TT, 0:P], maxes[:, cols], ident[:, :]).then_inc(x_full.sem, 1)

            def scores_by_key(b, h, c):
                if h % GH == 0 and c == 0:
                    shift_in.wait(pe, b, 16 * (h // GH + 1))
                u = h * KC + c
                ring_take(pe, free, "T", b, u)
                pe.matmul(ps_ring[:, ring_bank("T", u), :], k_stack[:, c * P:(c + 1) * P], q_stack[:, h, :],
                          start=True, stop=True).then_inc(full[ring_bank("T", u)], 1)

            def weighted(b, g, c):
                if c == 0:
                    ring_wait_all(pe, free, "T", b, (g + 1) * GH * KC - 1)
                    x_free.wait(pe, b, 1)
                    o_ok.wait(pe, b, g)
                for j in range(GH):
                    last = pe.matmul(ps_o[j * HD:(j + 1) * HD, :], val[:, c, :],
                                     probs[:, (g * GH + j) % (2 * GH), c, :], start=c == 0, stop=c == KC - 1)
                last.then_inc(pv_done.sem, 1)

            def sums(b, g, k):
                if k == 0:
                    pair_ok.wait(pe, b, (g + 1) * GH * 2)
                    rec_ok.wait(pe, b, g * TT)
                for j in range(GH):
                    last = pe.matmul(ps_sum[j * HD:(j + 1) * HD, :], ones[:, :], psums[:, j, k, :],
                                     start=k == 0, stop=k == 1)
                if k == 1:
                    last.then_inc(sum_done.sem, 1)

            def batch(b, first, last, ahead):
                for n in range(2 * GH * TT):
                    scores(b, n)
                    if n == GH * TT + 1:
                        max_rows(b, 0)
                    if not first:
                        for t, i in OUT_PLAN.get(n, ()):
                            out_product(b - 1, t, i)
                for s in range(H + 1):
                    g, j, p = s // GH, s % GH, projected(s)
                    if s == H:
                        for c in range(KC):
                            weighted(b, G - 1, c)
                            if c == 1:
                                sums(b, G - 1, 0)
                                sums(b, G - 1, 1)
                        if not last:
                            values(b + 1)
                        break
                    for c in range(KC):
                        if g < 2:
                            scores(b, ((g + 2) * GH + j) * TT + c)
                        if g >= 1 and j == 3 and c == 0:
                            weighted(b, g - 1, j)
                        scores_by_key(b, s, c)
                        if j == 0 and g + 1 < G and c == 1:
                            max_rows(b, g + 1)
                        if g >= 1 and (j, c) in SUMS_AT[g]:
                            sums(b, g - 1, SUMS_AT[g].index((j, c)))
                        if g >= 1 and j in (1, 2) and c == 1 or g >= 1 and j == 0 and c == 3:
                            weighted(b, g - 1, j)
                        if XT_SLOT <= s < XT_SLOT + 2 and c % 2 == 1 and not last:
                            transposes(b + 1, 2 * (s - XT_SLOT) + c // 2, False)
                        if 0 <= p < NQ and not last:
                            project(b + 1, p, c, KC)

            pe.wait_ge(w_lo_ok, 6)
            for c in range(KC):
                transposes(0, c, True)
            for p in range(NQ):
                project(0, p, 0, 1)
            values(0)
            batches(pe, batch)
            for plan in OUT_PLAN.values():
                for t, i in plan:
                    out_product(B - 1, t, i)


def rope_table():
    import numpy as np
    d = np.arange(P) % HD
    pos = np.float32(10000.0) ** ((np.float32(-2.0) * np.arange(0, HD, 2, dtype=np.float32) - np.float32(1.0))
                                  / np.float32(HD))
    angles = (np.arange(T, dtype=np.float32)[None, :] * pos[d % (HD // 2)][:, None]).astype(np.float32)
    sign = np.where(d < HD // 2, -1.0, 1.0).astype(np.float32)[:, None]
    return np.ascontiguousarray(np.stack([np.cos(angles), np.sin(angles) * sign], axis=1).astype(np.float32))


E, F = 8, 512
NT = B * T // P
ET = NT + E
RING4 = 4
REGION = B * T + P
NULL_ROW = E * REGION
SORTED_ROWS = NULL_ROW + P
ROW = 2 * D + 16
MATS = 3
EULER = 2.718281828459045


def experts(nc, x1, w_router, w_gate, w_up, w_down, ws_gate, ws_up, ws_down, rows, out):
    with ExitStack() as ctx:
        def sb(name, shape, dt=F32):
            return ctx.enter_context(nc.sbuf_tensor(name, shape, dt))

        def ps(name, cols=512):
            return ctx.enter_context(nc.psum_tensor(name, [P, 512], F32))

        def sem(name):
            return ctx.enter_context(nc.semaphore(name))

        w_hi = sb("w_hi", [P, 2, MATS, KC, F], F32R)
        w_lo = sb("w_lo", [P, 2, MATS, KC, F], F32R)
        raw = sb("raw", [P, MATS, KC, F])
        wr = sb("wr", [P, KC, E])
        wr_hi = sb("wr_hi", [P, KC, E], F32R)
        wr_lo = sb("wr_lo", [P, KC, E], F32R)
        identity = sb("identity", [P, P])
        before = sb("before", [P, P], BF16)
        all_ones = sb("all_ones", [P, P], BF16)
        first_wins = sb("first_wins", [P, E])
        region = sb("region", [P, E])
        minus_half = sb("minus_half", [P, 1])
        euler = sb("euler", [P, 1])
        token = sb("token", [P, 1])
        xt = sb("xt", [P, RING4, D])
        xn = sb("xn", [P, RING4, D])
        st = sb("st", [P, RING4, 6])
        mean_var = sb("mean_var", [P, RING4, 2])
        var_eps = sb("var_eps", [P, RING4])
        inv_std = sb("inv_std", [P, RING4])
        x_hi = sb("x_hi", [P, KC, P], F32R)
        x_lo = sb("x_lo", [P, KC, P], F32R)
        h_hi = sb("h_hi", [P, KC, P], F32R)
        h_lo = sb("h_lo", [P, KC, P], F32R)
        silu = sb("silu", [P, F])
        hid = sb("hid", [P, F])
        row = sb("row", [P, RING4, ROW])
        y_out = sb("y_out", [P, RING4, D])
        target = sb("target", [P, RING4], U32)
        logits = sb("logits", [P, E])
        top = sb("top", [P, 1])
        minus_top = sb("minus_top", [P, 1])
        exp_minus = sb("exp_minus", [P, 1])
        denom = sb("denom", [P, 1])
        score = sb("score", [P, 1])
        rank_of = sb("rank_of", [P, E])
        winner = sb("winner", [P, 1])
        chosen = sb("chosen", [P, E], BF16)
        chosen_so_far = sb("chosen_so_far", [P, E], BF16)
        place = sb("place", [P, E])
        place1 = sb("place1", [P, E])
        place_sum = sb("place_sum", [P, 1])
        mark_v = sb("mark_v", [P, 1])
        mark_p = sb("mark_p", [P, RING4 + 2])

        counts = sb("counts", [P, E])
        steps128 = sb("steps128", [P, E, NT])
        over = sb("over", [P, E, NT])
        tiles_of = sb("tiles_of", [P, E])
        tile_end = sb("tile_end", [P, E])
        jump = sb("jump", [P, E])
        tile_no = sb("tile_no", [P, ET, E])
        passed = sb("passed", [P, ET, E])
        weighted_p = sb("weighted_p", [P, ET, E])
        tabf = sb("tabf", [P, 6, ET])
        tab = sb("tab", [P, 5, ET], I32)
        EID, ODD, FIRST, BASE, FETCH, TMP = range(6)
        filler = sb("filler", [P, ROW])
        fill_at = sb("fill_at", [P, E])
        fill_row = sb("fill_row", [P, E], U32)
        lane = sb("lane", [P, 1])

        ps_g, ps_u, ps_xt, ps_ht, ps_y, ps_l, ps_k = (
            ps(f"ps_{n}") for n in ("g", "u", "xt", "ht", "y", "l", "k"))

        raw_in, fetched = sem("raw_in"), sem("fetched")
        wr_in, wr_ok = sem("wr_in"), sem("wr_ok")
        cst, cst_v = sem("cst"), sem("cst_v")
        sh_hi, sh_lo = sem("sh_hi"), sem("sh_lo")
        e_hi, e_lo = sem("e_hi"), sem("e_lo")
        marked = sem("marked")
        n_hi = sem("n_hi")
        n_lo = sem("n_lo")
        xt_in = [Counter(sem(f"xt_in{k}"), 16) for k in range(RING4)]
        row_io = [Counter(sem(f"row_io{k}"), 16) for k in range(RING4)]
        row_in = [Counter(sem(f"row_in{k}"), 16) for k in range(RING4)]
        y_io = [Counter(sem(f"y_io{k}"), 16) for k in range(RING4)]
        stat_ok = Counter(sem("stat_ok"), 3)
        inv_ok = Counter(sem("inv_ok"), 1)
        xn_ok = Counter(sem("xn_ok"), 1)
        g_full, u_full, x_full, h_full, y_full, l_full, k_full = (
            Counter(sem(f"{n}_full"), 1) for n in ("g", "u", "x", "h", "y", "l", "k"))
        silu_ok, xhi_ok, hhi_ok = (Counter(sem(n), 1) for n in ("silu_ok", "xhi_ok", "hhi_ok"))
        xlo_ok, hlo_ok, hid_ok, y_ok = (Counter(sem(n), 1) for n in ("xlo_ok", "hlo_ok", "hid_ok", "y_ok"))
        route = Counter(sem("route"), 6)
        exp_ok = Counter(sem("exp_ok"), 1)
        score_ok = Counter(sem("score_ok"), 2)
        xs_ok = Counter(sem("xs_ok"), 2)
        placed = Counter(sem("placed"), 5)
        token_ok = Counter(sem("token_ok"), 1)
        carried = Counter(sem("carried"), 1)
        table = sem("table")
        table_ok = sem("table_ok")
        count_ps, fill_io, fill_ok = sem("count_ps"), sem("fill_io"), sem("fill_ok")

        block = ctx.enter_context(nc.Block())

        def tiles(eng, t0, count, step):
            for k in range(RING4):
                step(t0 + k, k, k == 0, False)
            with eng.Fori(t0 // RING4 + 1, (t0 + count) // RING4 - 1) as i:
                for k in range(RING4):
                    step(i * RING4 + k, k, False, False)
            for k in range(RING4):
                step(t0 + count - RING4 + k, k, False, k == RING4 - 1)

        @contextmanager
        def next_weights(eng, t):
            j = t - NT
            new = eng.value_load(tab[0:1, FIRST, bass.ds(j, 1)], min_val=0, max_val=1)
            with eng.If(new > 0):
                e = eng.value_load(tab[0:1, EID, bass.ds(j, 1)], min_val=0, max_val=E - 1)
                odd = eng.value_load(tab[0:1, ODD, bass.ds(j, 1)], min_val=0, max_val=1)
                yield (e, lambda m: w_hi[:, bass.ds(1 - odd, 1), m, :, :].rearrange("p o c f -> p (o c f)"),
                       lambda m: w_lo[:, bass.ds(1 - odd, 1), m, :, :].rearrange("p o c f -> p (o c f)"),
                       lambda m: raw[:, m, :, :].rearrange("p c f -> p (c f)"))

        def ring_dma(eng, counters, t, k, done):
            v = (t - k) * (16 // RING4) + 16 * done
            if not isinstance(v, int) or v > 0:
                eng.wait_ge(counters[k].sem, v)

        @block.sync
        def _(sp):
            for m, w in enumerate((ws_gate, ws_up, ws_down)):
                sp.dma_start(raw[:, m, :, :], w.rearrange("(c p) n -> p c n", p=P)).then_inc(raw_in, 16)
            sp.dma_start(wr[:, :, :], w_router.rearrange("(c p) n -> p c n", p=P)).then_inc(wr_in, 16)

            def load_x(t, k, first, last):
                if not isinstance(t, int) or t >= RING4:
                    y_ok.wait(sp, t, 1 - RING4)
                sp.dma_start(xt[:, k, :], x1[bass.ds(t * P, P), :]).then_inc(xt_in[k].sem, 16)

            def load_row(t, k, first, last):
                j = t - NT
                at = sp.value_load(tab[0:1, BASE, bass.ds(j, 1)], min_val=0, max_val=NULL_ROW)
                y_ok.wait(sp, t, 1 - RING4)
                sp.dma_start(row[:, k, :], rows[bass.ds(at, P), :]).then_inc(row_in[k].sem, 16)

            for k in range(RING4):
                load_x(k, k, False, False)
            sp.wait_ge(sh_lo, MATS)
            for m, w in enumerate((w_gate, w_up, w_down)):
                sp.dma_start(raw[:, m, :, :], w[0, :, :].rearrange("(c p) n -> p c n", p=P)).then_inc(raw_in, 16)
            with sp.Fori(1, NT // RING4) as i:
                for k in range(RING4):
                    load_x(i * RING4 + k, k, False, False)
            sp.wait_ge(table_ok, 1)
            for k in range(RING4):
                sp.wait_ge(row_io[k].sem, 16 * (NT // RING4))
            sp.wait_ge(fill_io, 16 * (E + 1))
            tiles(sp, NT, ET, load_row)

        @block.gpsimd
        def _(pool):
            pool.memset(identity[:, :], 0.0).then_inc(cst, 1)
            pool.memset(before[:, :], 1.0).then_inc(cst, 1)
            pool.memset(all_ones[:, :], 1.0).then_inc(cst, 1)
            pool.memset(minus_half[:, :], -0.5).then_inc(cst, 1)
            pool.memset(euler[:, :], EULER).then_inc(cst, 1)
            pool.memset(mark_p[:, :], 0.0).then_inc(cst, 1)
            pool.memset(filler[:, :], 0.0).then_inc(cst, 1)
            pool.wait_ge(cst, 7)
            pool.affine_select(out=identity[:, :], in_=identity[:, :], compare_op=ALU.not_equal, fill=1.0,
                               base=0, pattern=[[-1, P]], channel_multiplier=1).then_inc(cst, 1)
            pool.affine_select(out=before[:, :], in_=before[:, :], compare_op=ALU.is_gt, fill=0.0,
                               base=0, pattern=[[1, P]], channel_multiplier=-1).then_inc(cst, 1)
            pool.iota(first_wins[:, :], [[-1, E]], base=E, channel_multiplier=0,
                      allow_small_or_imprecise_dtypes=True).then_inc(cst, 1)
            pool.iota(region[:, :], [[REGION, E]], base=0, channel_multiplier=0,
                      allow_small_or_imprecise_dtypes=True).then_inc(cst, 1)
            pool.iota(token[:, :], [[0, 1]], base=0, channel_multiplier=1,
                      allow_small_or_imprecise_dtypes=True).then_inc(cst, 1)
            pool.iota(lane[:, :], [[0, 1]], base=0, channel_multiplier=1,
                      allow_small_or_imprecise_dtypes=True).then_inc(cst, 1)
            pool.iota(steps128[:, :, :], [[0, E], [P, NT]], base=0, channel_multiplier=0,
                      allow_small_or_imprecise_dtypes=True).then_inc(cst, 1)
            pool.iota(tile_no[:, :, :], [[1, ET], [0, E]], base=0, channel_multiplier=0,
                      allow_small_or_imprecise_dtypes=True).then_inc(cst, 1)
            pool.wait_ge(cst, 15)
            pool.iota(filler[:, 2 * D:2 * D + 1], [[0, 1]], base=B * T, channel_multiplier=1,
                      allow_small_or_imprecise_dtypes=True).then_inc(cst, 1)
            pool.wait_ge(cst, 16)

            def norm_power(t, k):
                stat_ok.wait(pool, t, 3)
                pool.tensor_tensor(inv_std[:, k:k + 1], var_eps[:, k:k + 1], minus_half[:, :],
                                   ALU.pow).then_inc(inv_ok.sem, 1)

            PIECE = MATS * KC * F // (NT // RING4)
            raw_flat = raw[:, :, :, :].rearrange("p m c f -> p (m c f)")
            hi_flat = w_hi[:, 0, :, :, :].rearrange("p m c f -> p (m c f)")
            lo_flat = w_lo[:, 0, :, :, :].rearrange("p m c f -> p (m c f)")

            def piece(i):
                cols = bass.ds(i * PIECE, PIECE)
                pool.tensor_copy(hi_flat[:, cols], raw_flat[:, cols]).then_inc(e_hi, 1)
                pool.wait_ge(e_hi, i + 1)
                pool.tensor_tensor(lo_flat[:, cols], raw_flat[:, cols], hi_flat[:, cols].bitcast(F32),
                                   ALU.subtract).then_inc(e_lo, 1)

            def shared_step(t, k, first, last):
                route.wait(pool, t, 6)
                pool.tensor_tensor(exp_minus[:, :], euler[:, :], minus_top[:, :], ALU.pow).then_inc(exp_ok.sem, 1)
                if k == 2:
                    if isinstance(t, int) and t < RING4:
                        pool.wait_ge(raw_in, 16 * 2 * MATS)
                    piece((t - 2) // RING4 if isinstance(t, int) else it[0])
                if not last and not (isinstance(t, int) and t + 2 >= NT):
                    norm_power(t + 2, (k + 2) % RING4)
                if not first:
                    scatter(t - 1, (k - 1) % RING4)

            def scatter(t, k):
                placed.wait(pool, t, 5)
                xs_ok.wait(pool, t, 2)
                y_ok.wait(pool, t, 1)
                carried.wait(pool, t, 1 - RING4)
                pool.tensor_tensor(mark_p[:, k:k + 1], euler[:, :], euler[:, :], ALU.add).then_inc(carried.sem, 1)
                pool.indirect_dma_start(out=rows, out_offset=bass.IndirectOffsetOnAxis(ap=target[:, k:k + 1], axis=0),
                                        in_=row[:, k, :], in_offset=None).then_inc(row_io[k].sem, 16)

            norm_power(0, 0)
            norm_power(1, 1)
            it = [None]
            for k in range(RING4):
                shared_step(k, k, k == 0, False)
            with pool.Fori(1, NT // RING4 - 1) as i:
                it[0] = i
                for k in range(RING4):
                    shared_step(i * RING4 + k, k, False, False)
            for k in range(RING4):
                shared_step(NT - RING4 + k, k, False, k == RING4 - 1)
            scatter(NT - 1, RING4 - 1)
            pool.wait_ge(e_lo, NT // RING4)
            for m, w in enumerate((w_gate, w_up, w_down)):
                pool.dma_start(raw[:, m, :, :], w[1, :, :].rearrange("(c p) n -> p c n", p=P)).then_inc(fetched, 16)
            pool.wait_ge(fill_ok, 1)
            for k in range(RING4):
                pool.wait_ge(row_io[k].sem, 16 * (NT // RING4))
            for e in range(E):
                pool.indirect_dma_start(out=rows, out_offset=bass.IndirectOffsetOnAxis(ap=fill_row[:, e:e + 1], axis=0),
                                        in_=filler[:, :], in_offset=None).then_inc(fill_io, 16)
            pool.dma_start(rows[NULL_ROW:NULL_ROW + P, :], filler[:, :]).then_inc(fill_io, 16)
            pool.wait_ge(table_ok, 1)
            pool.tensor_tensor(mark_p[:, RING4:RING4 + 1], euler[:, :], euler[:, :], ALU.add).then_inc(marked, 1)
            pool.tensor_tensor(mark_p[:, 0:1], euler[:, :], euler[:, :], ALU.add).then_inc(n_lo, 1)

            def expert_step(t, k, first, last):
                j = t - NT
                with next_weights(pool, t) as (e, hi, lo, src):
                    for m in range(MATS):
                        pool.wait_ge(n_hi, e * MATS + m + 1)
                        if m == 0:
                            pool.tensor_tensor(mark_p[:, RING4 + 1:], euler[:, :], euler[:, :], ALU.add)
                        pool.tensor_tensor(lo(m), src(m), hi(m).bitcast(F32), ALU.subtract).then_inc(n_lo, 1)
                    pool.wait_ge(marked, 1 + e)
                    pool.wait_ge(n_lo, 1 + (e + 1) * MATS)
                    pool.tensor_tensor(mark_p[:, RING4:RING4 + 1], euler[:, :], euler[:, :], ALU.add)                         .then_inc(marked, 1)
                    nxt = pool.value_load(tab[0:1, FETCH, bass.ds(j, 1)], min_val=0, max_val=E - 1)
                    for m, w in enumerate((w_gate, w_up, w_down)):
                        pool.dma_start(raw[:, m, :, :], w[bass.ds(nxt, 1), :, :]
                                       .rearrange("o (c p) n -> p (o c) n", p=P)).then_inc(fetched, 16)
                if not first:
                    deliver(t - 1, (k - 1) % RING4)

            def deliver(t, k):
                y_ok.wait(pool, t, 1)
                carried.wait(pool, t, 1 - RING4)
                pool.tensor_tensor(mark_p[:, k:k + 1], euler[:, :], euler[:, :], ALU.add).then_inc(carried.sem, 1)
                pool.indirect_dma_start(out=out, out_offset=bass.IndirectOffsetOnAxis(ap=target[:, k:k + 1], axis=0),
                                        in_=y_out[:, k, :], in_offset=None, bounds_check=B * T - 1,
                                        oob_is_err=False).then_inc(y_io[k].sem, 16)

            tiles(pool, NT, ET, expert_step)
            deliver(NT + ET - 1, RING4 - 1)
            for k in range(RING4):
                pool.wait_ge(y_io[k].sem, 16 * (ET // RING4))
            pool.wait_ge(fetched, 16 * MATS * E)

        @block.scalar
        def _(act):
            def copy(out_, in_):
                return act.activation(out_, in_, ACT.Copy)

            for m in range(MATS):
                act.wait_ge(raw_in, 16 * MATS)
                copy(w_hi[:, 1, m, :, :], raw[:, m, :, :]).then_inc(sh_hi, 1)
            act.wait_ge(wr_in, 16)
            copy(wr_hi[:, :, :], wr[:, :, :]).then_inc(wr_ok, 1)

            def high_x(t):
                x_full.wait(act, t, 1)
                copy(x_hi[:, :, :], ps_xt[:, :].rearrange("p (c t) -> p c t", t=P)).then_inc(xhi_ok.sem, 1)

            def high_h(t):
                h_full.wait(act, t, 1)
                y_full.wait(act, t, 0)
                copy(h_hi[:, :, :], ps_ht[:, :].rearrange("p (c t) -> p c t", t=P)).then_inc(hhi_ok.sem, 1)

            def step(t, k, first, last):
                g_full.wait(act, t, 1)
                hid_ok.wait(act, t, 0)
                act.activation(silu[:, :], ps_g[:, :], ACT.Silu).then_inc(silu_ok.sem, 1)
                if not first:
                    high_h(t - 1)
                if not last:
                    high_x(t + 1)

            def expert_step(t, k, first, last):
                step(t, k, first, last)
                with next_weights(act, t) as (e, hi, lo, src):
                    act.wait_ge(y_full.sem, t)
                    act.wait_ge(fetched, (e + 1) * 16 * MATS)
                    for m in range(MATS):
                        copy(hi(m), src(m)).then_inc(n_hi, 1)

            high_x(0)
            tiles(act, 0, NT, step)
            high_h(NT - 1)
            high_x(NT)
            act.wait_ge(table_ok, 1)
            tiles(act, NT, ET, expert_step)
            high_h(NT + ET - 1)

        @block.vector
        def _(dve):
            def minus(o, a, b):
                return dve.tensor_tensor(o, a, b.bitcast(F32), ALU.subtract)

            dve.memset(chosen_so_far[:, :], 0.0).then_inc(cst_v, 1)

            def stats_of(t, k):
                ring_dma(dve, xt_in, t, k, 1)
                dve.bn_stats(st[:, k, :], xt[:, k, :]).then_inc(stat_ok.sem, 1)
                stat_ok.wait(dve, t, 1)
                dve.memset(mark_v[:, :], 0.0)
                dve.bn_aggr(mean_var[:, k, :], st[:, k, :]).then_inc(stat_ok.sem, 1)
                stat_ok.wait(dve, t, 2)
                dve.tensor_scalar(var_eps[:, k:k + 1], mean_var[:, k, 1:2], EPS, None, ALU.add) \
                    .then_inc(stat_ok.sem, 1)

            def normalise(t, k):
                inv_ok.wait(dve, t, 1)
                dve.tensor_scalar(xn[:, k, :], xt[:, k, :], mean_var[:, k, 0:1], inv_std[:, k:k + 1],
                                  ALU.subtract, ALU.mult).then_inc(xn_ok.sem, 1)

            def low_x(t):
                xhi_ok.wait(dve, t, 1)
                minus(x_lo[:, :, :], ps_xt[:, :].rearrange("p (c t) -> p c t", t=P),
                      x_hi[:, :, :]).then_inc(xlo_ok.sem, 1)

            def low_h(t):
                hhi_ok.wait(dve, t, 1)
                minus(h_lo[:, :, :], ps_ht[:, :].rearrange("p (c t) -> p c t", t=P),
                      h_hi[:, :, :]).then_inc(hlo_ok.sem, 1)

            def hidden(t):
                silu_ok.wait(dve, t, 1)
                u_full.wait(dve, t, 1)
                h_full.wait(dve, t, 0)
                dve.tensor_tensor(hid[:, :], ps_u[:, :], silu[:, :], ALU.mult).then_inc(hid_ok.sem, 1)

            def choose(t):
                l_full.wait(dve, t, 1)
                dve.tensor_copy(logits[:, :], ps_l[:, 0:E]).then_inc(route.sem, 1)
                route.wait(dve, t, 1)
                dve.tensor_reduce(top[:, :], logits[:, :], AX.X, ALU.max).then_inc(route.sem, 1)
                route.wait(dve, t, 2)
                dve.scalar_tensor_tensor(rank_of[:, :], logits[:, :], top[:, 0:1], first_wins[:, :],
                                         ALU.is_equal, ALU.mult).then_inc(route.sem, 1)
                route.wait(dve, t, 3)
                dve.tensor_reduce(winner[:, :], rank_of[:, :], AX.X, ALU.max).then_inc(route.sem, 1)
                route.wait(dve, t, 4)
                placed.wait(dve, t, 0)
                dve.tensor_scalar(chosen[:, :], rank_of[:, :], winner[:, 0:1], None, ALU.is_equal) \
                    .then_inc(route.sem, 1)
                dve.tensor_scalar(minus_top[:, :], top[:, :], -1.0, None, ALU.mult).then_inc(route.sem, 1)

            def scale(t, k):
                exp_ok.wait(dve, t, 1)
                dve.tensor_scalar(denom[:, :], exp_minus[:, :], 1.0, None, ALU.add).then_inc(score_ok.sem, 1)
                score_ok.wait(dve, t, 1)
                dve.reciprocal(score[:, :], denom[:, :]).then_inc(score_ok.sem, 1)
                score_ok.wait(dve, t, 2)
                ring_dma(dve, row_io, t, k, 0)
                dve.tensor_scalar(row[:, k, 0:D], xn[:, k, :], score[:, 0:1], None, ALU.mult) \
                    .then_inc(xs_ok.sem, 1)
                token_ok.wait(dve, t, 0)
                dve.tensor_scalar(row[:, k, 2 * D:ROW], filler[:, 2 * D:ROW], 0.0, token[:, 0:1],
                                  ALU.mult, ALU.add).then_inc(xs_ok.sem, 1)

            def put(t, k):
                k_full.wait(dve, t, 1)
                dve.tensor_tensor(place[:, :], ps_k[:, 0:E], region[:, :], ALU.add).then_inc(placed.sem, 1)
                placed.wait(dve, t, 1)
                dve.tensor_tensor(place1[:, :], place[:, :], chosen[:, :], ALU.mult).then_inc(placed.sem, 1)
                placed.wait(dve, t, 2)
                dve.tensor_reduce(place_sum[:, :], place1[:, :], AX.X, ALU.add).then_inc(placed.sem, 1)
                placed.wait(dve, t, 3)
                ring_dma(dve, row_io, t, k, 0)
                dve.tensor_copy(target[:, k:k + 1], place_sum[:, :]).then_inc(placed.sem, 1)
                dve.tensor_tensor(chosen_so_far[:, :], chosen_so_far[:, :], chosen[:, :],
                                  ALU.add).then_inc(placed.sem, 1)

            def shared_out(t, k):
                y_full.wait(dve, t, 1)
                dve.tensor_tensor(row[:, k, D:2 * D], ps_y[:, :], xt[:, k, :], ALU.add).then_inc(y_ok.sem, 1)
                xs_ok.wait(dve, t, 2)
                dve.tensor_scalar(token[:, :], token[:, :], float(P), None, ALU.add).then_inc(token_ok.sem, 1)

            def shared_step(t, k, first, last):
                if not first:
                    low_h(t - 1)
                    put(t - 1, (k - 1) % RING4)
                hidden(t)
                choose(t)
                if not last:
                    low_x(t + 1)
                if not first:
                    shared_out(t - 1, (k - 1) % RING4)
                if not (isinstance(t, int) and t + 2 >= NT):
                    stats_of(t + 2, (k + 2) % RING4)
                scale(t, k)
                if not (isinstance(t, int) and t + 2 >= NT):
                    normalise(t + 2, (k + 2) % RING4)

            stats_of(0, 0)
            stats_of(1, 1)
            for m in range(MATS):
                dve.wait_ge(sh_hi, m + 1)
                minus(w_lo[:, 1, m, :, :], raw[:, m, :, :], w_hi[:, 1, m, :, :]).then_inc(sh_lo, 1)
            dve.wait_ge(wr_ok, 1)
            minus(wr_lo[:, :, :], wr[:, :, :], wr_hi[:, :, :]).then_inc(wr_ok, 1)
            dve.wait_ge(cst, 16)
            normalise(0, 0)
            normalise(1, 1)
            low_x(0)
            tiles(dve, 0, NT, shared_step)
            low_h(NT - 1)
            put(NT - 1, RING4 - 1)
            shared_out(NT - 1, RING4 - 1)

            n_table = [0]

            def link(ins):
                ins.then_inc(table, 1)
                n_table[0] += 1
                dve.wait_ge(table, n_table[0])

            dve.wait_ge(count_ps, 1)
            link(dve.tensor_copy(counts[:, :], ps_k[:, 0:E]))
            link(dve.tensor_tensor(fill_at[:, :], counts[:, :], region[:, :], ALU.add))
            link(dve.tensor_scalar(fill_at[:, :], fill_at[:, :], lane[:, 0:1], None, ALU.add))
            dve.tensor_copy(fill_row[:, :], fill_at[:, :]).then_inc(fill_ok, 1)
            link(dve.tensor_tensor(over[:, :, :], counts[:, :].rearrange("p (e o) -> p e o", o=1)
                                   .to_broadcast([P, E, NT]), steps128[:, :, :], ALU.is_gt))
            link(dve.tensor_reduce(tiles_of[:, :], over[:, :, :], AX.X, ALU.add))
            link(dve.tensor_scalar(tiles_of[:, :], tiles_of[:, :], 1.0, None, ALU.max))
            link(dve.tensor_scalar(jump[:, :], tiles_of[:, :], -float(P), float(REGION), ALU.mult, ALU.add))
            link(dve.tensor_copy(tile_end[:, :], tiles_of[:, :]))
            for e in range(1, E):
                link(dve.tensor_tensor(tile_end[:, e:e + 1], tile_end[:, e - 1:e], tile_end[:, e:e + 1], ALU.add))
            link(dve.tensor_tensor(passed[:, :, :], tile_no[:, :, :],
                                   tile_end[:, :].rearrange("p (o e) -> p o e", o=1).to_broadcast([P, ET, E]),
                                   ALU.is_ge))
            link(dve.tensor_tensor(weighted_p[:, :, :], passed[:, :, :],
                                   jump[:, :].rearrange("p (o e) -> p o e", o=1).to_broadcast([P, ET, E]),
                                   ALU.mult))
            link(dve.tensor_reduce(tabf[:, EID, :], passed[:, :, 0:E - 1], AX.X, ALU.add))
            link(dve.tensor_reduce(tabf[:, BASE, :], weighted_p[:, :, :], AX.X, ALU.add))
            link(dve.scalar_tensor_tensor(tabf[:, BASE, :], tile_no[:, :, 0], float(P), tabf[:, BASE, :],
                                          ALU.mult, ALU.add))
            link(dve.tensor_scalar(tabf[:, BASE, :], tabf[:, BASE, :], float(NULL_ROW), None, ALU.min))
            link(dve.tensor_reduce(tabf[:, TMP, :], passed[:, :, 1:E - 1:2], AX.X, ALU.add))
            link(dve.scalar_tensor_tensor(tabf[:, ODD, :], tabf[:, TMP, :], -2.0, tabf[:, EID, :],
                                          ALU.mult, ALU.add))
            link(dve.memset(tabf[:, FIRST, 0:1], 1.0))
            link(dve.tensor_tensor(tabf[:, FIRST, 1:ET], tabf[:, EID, 1:ET], tabf[:, EID, 0:ET - 1], ALU.subtract))
            link(dve.tensor_scalar(tabf[:, TMP, :], tabf[:, EID, :], float(E - 1), None, ALU.is_lt))
            link(dve.tensor_tensor(tabf[:, FIRST, :], tabf[:, FIRST, :], tabf[:, TMP, :], ALU.mult))
            link(dve.tensor_scalar(tabf[:, FETCH, :], tabf[:, EID, :], 2.0, float(E - 1), ALU.add, ALU.min))
            dve.tensor_copy(tab[:, :, :], tabf[:, 0:5, :]).then_inc(table_ok, 1)

            def expert_out(t, k):
                y_full.wait(dve, t, 1)
                ring_dma(dve, y_io, t - NT, k, 0)
                dve.tensor_copy(target[:, k:k + 1], row[:, k, 2 * D:2 * D + 1])
                dve.tensor_tensor(y_out[:, k, :], ps_y[:, :], row[:, k, D:2 * D], ALU.add).then_inc(y_ok.sem, 1)

            def expert_step(t, k, first, last):
                if not first:
                    low_h(t - 1)
                hidden(t)
                if not last:
                    low_x(t + 1)
                if not first:
                    expert_out(t - 1, (k - 1) % RING4)

            low_x(NT)
            tiles(dve, NT, ET, expert_step)
            low_h(NT + ET - 1)
            expert_out(NT + ET - 1, RING4 - 1)

        @block.tensor
        def _(pe):
            pe.wait_ge(cst, 16)
            pe.wait_ge(cst_v, 1)

            def weights(m, c, s):
                if isinstance(s, int):
                    return w_hi[:, s, m, c, :], w_lo[:, s, m, c, :]
                at = bass.ds(s, 1)
                return (w_hi[:, at, m, c, :].rearrange("p o f -> p (o f)"),
                        w_lo[:, at, m, c, :].rearrange("p o f -> p (o f)"))

            def transpose_x(t, k):
                xlo_ok.wait(pe, t, 0)
                if shared[0]:
                    xn_ok.wait(pe, t, 1)
                    src = xn
                else:
                    ring_dma(pe, row_in, t - NT, k, 1)
                    src = row
                for c in range(KC):
                    last = pe.transpose(ps_xt[:, c * P:(c + 1) * P], src[:, k, c * P:(c + 1) * P], identity[:, :])
                last.then_inc(x_full.sem, 1)

            def gate(t, s):
                xlo_ok.wait(pe, t, 1)
                silu_ok.wait(pe, t, 0)
                products(pe, ps_g[:, :], [((x_hi[:, c, :], x_lo[:, c, :]), weights(0, c, s))
                                          for c in range(KC)]).then_inc(g_full.sem, 1)

            def up(t, s):
                hid_ok.wait(pe, t, 0)
                products(pe, ps_u[:, :], [((x_hi[:, c, :], x_lo[:, c, :]), weights(1, c, s))
                                          for c in range(KC)]).then_inc(u_full.sem, 1)

            def transpose_h(t):
                hid_ok.wait(pe, t, 1)
                hlo_ok.wait(pe, t, 0)
                for c in range(KC):
                    last = pe.transpose(ps_ht[:, c * P:(c + 1) * P], hid[:, c * P:(c + 1) * P], identity[:, :])
                last.then_inc(h_full.sem, 1)

            def down(t, s):
                hlo_ok.wait(pe, t, 1)
                y_ok.wait(pe, t, 0)
                products(pe, ps_y[:, :], [((h_hi[:, c, :], h_lo[:, c, :]), weights(2, c, s))
                                          for c in range(KC)]).then_inc(y_full.sem, 1)

            def router(t):
                route.wait(pe, t, -5)
                products(pe, ps_l[:, 0:E], [((x_hi[:, c, :], x_lo[:, c, :]), (wr_hi[:, c, :], wr_lo[:, c, :]))
                                            for c in range(KC)]).then_inc(l_full.sem, 1)

            def ranks(t):
                route.wait(pe, t, 5)
                placed.wait(pe, t, 0)
                pe.matmul(ps_k[:, 0:E], before[:, :], chosen[:, :], start=True, stop=False)
                pe.matmul(ps_k[:, 0:E], all_ones[:, :], chosen_so_far[:, :], start=False,
                          stop=True).then_inc(k_full.sem, 1)

            def shared_step(t, k, first, last):
                gate(t, 1)
                if not first:
                    ranks(t - 1)
                    transpose_h(t - 1)
                up(t, 1)
                router(t)
                if not last:
                    transpose_x(t + 1, (k + 1) % RING4)
                if not first:
                    down(t - 1, 1)

            shared = [True]
            pe.wait_ge(sh_lo, MATS)
            pe.wait_ge(wr_ok, 2)
            transpose_x(0, 0)
            tiles(pe, 0, NT, shared_step)
            ranks(NT - 1)
            transpose_h(NT - 1)
            down(NT - 1, 1)
            placed.wait(pe, NT, 0)
            pe.matmul(ps_k[:, 0:E], all_ones[:, :], chosen_so_far[:, :], start=True, stop=True).then_inc(count_ps, 1)
            pe.wait_ge(table_ok, 1)

            def expert_step(t, k, first, last):
                j = t - NT
                e = pe.value_load(tab[0:1, EID, bass.ds(j, 1)], min_val=0, max_val=E - 1)
                s = pe.value_load(tab[0:1, ODD, bass.ds(j, 1)], min_val=0, max_val=1)
                pe.wait_ge(n_lo, 1 + e * MATS)
                gate(t, s)
                if not first:
                    transpose_h(t - 1)
                up(t, s)
                if not last:
                    transpose_x(t + 1, (k + 1) % RING4)
                if not first:
                    s0 = pe.value_load(tab[0:1, ODD, bass.ds(j - 1, 1)], min_val=0, max_val=1)
                    down(t - 1, s0)

            shared[0] = False
            pe.wait_ge(e_lo, NT // RING4)
            transpose_x(NT, 0)
            tiles(pe, NT, ET, expert_step)
            transpose_h(NT + ET - 1)
            s = pe.value_load(tab[0:1, ODD, ET - 1:ET], min_val=0, max_val=1)
            down(NT + ET - 1, s)


_INS = ['L0_attn_x', 'L0_attn_w_attn', 'L0_attn_w_out', 'L0_ffn_router_w', 'L0_ffn_gate_w', 'L0_ffn_up_w',
        'L0_ffn_down_w', 'L0_ffn_shared_gate_w', 'L0_ffn_shared_up_w', 'L0_ffn_shared_down_w']


def kernel(**inputs):
    import numpy as _np
    import concourse.bacc as _bacc
    from concourse.bass_utils import run_bass_kernel_spmd as _run

    nc = _bacc.Bacc("TRN2", target_bir_lowering=False, num_devices=1)
    arrays, args = {}, []
    for name in _INS:
        a = _np.ascontiguousarray(inputs[name])
        arrays[f"in_{name}_dram"] = a
        args.append(nc.dram_tensor(f"in_{name}_dram", a.shape, mybir.dt.from_np(a.dtype), kind="ExternalInput").ap())
    arrays["rope"] = rope_table()
    rope = nc.dram_tensor("rope", arrays["rope"].shape, F32, kind="ExternalInput").ap()
    q_dram = nc.dram_tensor("q_dram", (B, G, 2, P, T), F32, kind="Internal").ap()
    x1 = nc.dram_tensor("x1_dram", (B * T, D), F32, kind="Internal").ap()
    rows = nc.dram_tensor("rows_dram", (SORTED_ROWS, ROW), F32, kind="Internal").ap()
    out = nc.dram_tensor("out_0_dram", (B * T, D), F32, kind="ExternalOutput").ap()
    x, w_attn, w_out, *ffn = args
    attention(nc, x, w_attn, w_out, rope, q_dram, x1)
    experts(nc, x1, *ffn, rows, out)
    r = _run(nc, [arrays], core_ids=[0])
    return r.results[0]["out_0_dram"].reshape(B, T, D)
```
